# Optimizing a Trainium2 kernel written in Bass

```python
import numpy as np
import jax
import jax.numpy as jnp

def _softmax(x, axis=-1):
    return jax.nn.softmax(x, axis=axis)
def _gelu(x):
    return jax.nn.gelu(x, approximate=True)
def _silu(x):
    return jax.nn.silu(x)
def _sigmoid(x):
    return jax.nn.sigmoid(x)
def _layernorm(x, axis=-1, eps=1e-5):
    m = jnp.mean(x, axis=axis, keepdims=True)
    v = jnp.var(x, axis=axis, keepdims=True)
    return (x - m) / jnp.sqrt(v + eps)
def _scatter_add(tgt, idx, src, axis=0):
    return tgt.at[idx].add(src)
def _segment_sum(src, seg, n):
    return jax.ops.segment_sum(src, seg, n)

kernel_name = 'mk_metaformer_d1_conv_nhwc512_7bcb44'

def setup_inputs(seed: int = 0):
    np.random.seed(seed)
    _w = jnp.asarray
    def _rec_inputs():
        import jax
        import jax.numpy as jnp
        _gk = jax.random.key(seed)
        x = -0.0002023 + 1 * jax.random.normal(jax.random.fold_in(_gk, 1), (64, 14, 14, 512), jnp.float32)
        return x
    x = _rec_inputs()
    def _L0_conv_setup():
        import jax, jax.numpy as jnp
        import numpy as np
        EPS = 1e-06
        NUM_HEADS = 8
        GAMMA = 0.999

        def simple_rms_norm(x):
            return x * jax.lax.rsqrt(jnp.mean(x * x, axis=-1, keepdims=True) + EPS)

        def gtu2d_forward(x, Wu, bu, Wv, bv, Wo, bo, rpe_pos_w, rpe_pos_b, rpe_w1, rpe_b1, rpe_w2, rpe_b2, rpe_w3, rpe_b3, rpe_out_w, rpe_out_b):
            B, n, m, E = x.shape
            d1 = Wu.shape[1]
            hd = d1 // NUM_HEADS
            u = jax.nn.silu(x @ Wu + bu)
            v = jax.nn.silu(x @ Wv + bv)
            v = v.reshape(B, n, m, NUM_HEADS, hd).transpose(0, 3, 1, 2, 4)
            ii = jnp.arange(-(n - 1), n, dtype=jnp.float32)
            jj = jnp.arange(-(m - 1), m, dtype=jnp.float32)
            pos = jnp.stack(jnp.meshgrid(ii, jj, indexing='ij'), axis=-1)
            r = pos @ rpe_pos_w + rpe_pos_b
            for w, b in ((rpe_w1, rpe_b1), (rpe_w2, rpe_b2), (rpe_w3, rpe_b3)):
                r = jax.nn.relu(simple_rms_norm(r)) @ w + b
            r = jax.nn.relu(simple_rms_norm(r)) @ rpe_out_w + rpe_out_b
            a = r.reshape(2 * n - 1, 2 * m - 1, NUM_HEADS, hd).transpose(2, 0, 1, 3)
            dist = jnp.abs(pos[..., 0]) + jnp.abs(pos[..., 1])
            a = a * (GAMMA ** dist)[None, :, :, None]
            t = jnp.zeros((NUM_HEADS, 2 * n, 2 * m, hd), a.dtype)
            t = t.at[:, :n, :m].set(a[:, n - 1:, m - 1:])
            t = t.at[:, n + 1:, :m].set(a[:, :n - 1, m - 1:])
            t = t.at[:, :n, m + 1:].set(a[:, n - 1:, :m - 1])
            t = t.at[:, n + 1:, m + 1:].set(a[:, :n - 1, :m - 1])
            xf = jnp.fft.rfft2(v, s=(2 * n, 2 * m), axes=(2, 3))
            tf = jnp.fft.rfft2(t, s=(2 * n, 2 * m), axes=(1, 2))
            y = jnp.fft.irfft2(xf * tf[None], s=(2 * n, 2 * m), axes=(2, 3))[:, :, :n, :m, :]
            y = y.transpose(0, 2, 3, 1, 4).reshape(B, n, m, d1)
            return u * y @ Wo + bo
        key = jax.random.key(seed)
        ks = jax.random.split(key, 12)
        B, N, M, E = (64, 14, 14, 512)
        D1 = 2 * E
        RPE = 512
        s = 0.02
        inp = {'x': jax.random.normal(ks[0], (B, N, M, E), jnp.float32), 'H': N, 'W': M, 'Wu': jax.random.normal(ks[1], (E, D1), jnp.float32) * s, 'bu': jnp.zeros((D1,), jnp.float32), 'Wv': jax.random.normal(ks[2], (E, D1), jnp.float32) * s, 'bv': jnp.zeros((D1,), jnp.float32), 'Wo': jax.random.normal(ks[3], (D1, E), jnp.float32) * s, 'bo': jnp.zeros((E,), jnp.float32), 'rpe_pos_w': jax.random.normal(ks[4], (2, RPE), jnp.float32) * s, 'rpe_pos_b': jnp.zeros((RPE,), jnp.float32), 'rpe_w1': jax.random.normal(ks[5], (RPE, RPE), jnp.float32) * s, 'rpe_b1': jnp.zeros((RPE,), jnp.float32), 'rpe_w2': jax.random.normal(ks[6], (RPE, RPE), jnp.float32) * s, 'rpe_b2': jnp.zeros((RPE,), jnp.float32), 'rpe_w3': jax.random.normal(ks[7], (RPE, RPE), jnp.float32) * s, 'rpe_b3': jnp.zeros((RPE,), jnp.float32), 'rpe_out_w': jax.random.normal(ks[8], (RPE, D1), jnp.float32) * s, 'rpe_out_b': jnp.zeros((D1,), jnp.float32)}
        return inp
    _L0_conv_all = _L0_conv_setup()
    _L0_conv_in = {k: v for k, v in _L0_conv_all.items() if k in ('Wu', 'bu', 'Wv', 'bv', 'Wo', 'bo', 'rpe_pos_w', 'rpe_pos_b', 'rpe_w1', 'rpe_b1', 'rpe_w2', 'rpe_b2', 'rpe_w3', 'rpe_b3', 'rpe_out_w', 'rpe_out_b', )}
    del _L0_conv_all

    def _L0_ffn_setup():
        import jax, jax.numpy as jnp
        import numpy as np

        def _haar_dwt2(x):
            a = x[:, ::2, ::2]
            b = x[:, ::2, 1::2]
            c = x[:, 1::2, ::2]
            d = x[:, 1::2, 1::2]
            ll = (a + b + c + d) * 0.5
            lh = (a + b - c - d) * 0.5
            hl = (a - b + c - d) * 0.5
            hh = (a - b - c + d) * 0.5
            return (ll, lh, hl, hh)

        def _haar_idwt2(ll, lh, hl, hh):
            a = (ll + lh + hl + hh) * 0.5
            b = (ll + lh - hl - hh) * 0.5
            c = (ll - lh + hl - hh) * 0.5
            d = (ll - lh - hl + hh) * 0.5
            B, H2, W2 = ll.shape
            out = jnp.zeros((B, 2 * H2, 2 * W2), ll.dtype)
            out = out.at[:, ::2, ::2].set(a)
            out = out.at[:, ::2, 1::2].set(b)
            out = out.at[:, 1::2, ::2].set(c)
            out = out.at[:, 1::2, 1::2].set(d)
            return out

        def _interp_linear_last(x, m):
            n = x.shape[-1]
            pos = jnp.linspace(0.0, 1.0, m, dtype=x.dtype) * (n - 1)
            i0 = jnp.clip(jnp.floor(pos).astype(jnp.int32), 0, n - 2)
            w = pos - i0.astype(x.dtype)
            return x[..., i0] * (1.0 - w) + x[..., i0 + 1] * w
        key = jax.random.key(seed)
        k0, k1, k2 = jax.random.split(key, 3)
        b, f, c, hidden = (128, 256, 512, 2048)
        x = jax.random.normal(k0, (b, f, c), dtype=jnp.float32)
        fc1_w = jax.random.normal(k1, (hidden, c), dtype=jnp.float32) * 0.02
        fc1_b = jnp.zeros((hidden,), dtype=jnp.float32)
        fc2_w = jax.random.normal(k2, (c // 2, hidden), dtype=jnp.float32) * 0.02
        fc2_b = jnp.zeros((c // 2,), dtype=jnp.float32)
        return {'x': x, 'fc1_w': fc1_w, 'fc1_b': fc1_b, 'fc2_w': fc2_w, 'fc2_b': fc2_b}
    _L0_ffn_all = _L0_ffn_setup()
    _L0_ffn_in = {k: v for k, v in _L0_ffn_all.items() if k in ('fc1_w', 'fc1_b', 'fc2_w', 'fc2_b', )}
    del _L0_ffn_all

    return {
        "x": x,
        "L0_conv_Wu": _L0_conv_in["Wu"],
        "L0_conv_bu": _L0_conv_in["bu"],
        "L0_conv_Wv": _L0_conv_in["Wv"],
        "L0_conv_bv": _L0_conv_in["bv"],
        "L0_conv_Wo": _L0_conv_in["Wo"],
        "L0_conv_bo": _L0_conv_in["bo"],
        "L0_conv_rpe_pos_w": _L0_conv_in["rpe_pos_w"],
        "L0_conv_rpe_pos_b": _L0_conv_in["rpe_pos_b"],
        "L0_conv_rpe_w1": _L0_conv_in["rpe_w1"],
        "L0_conv_rpe_b1": _L0_conv_in["rpe_b1"],
        "L0_conv_rpe_w2": _L0_conv_in["rpe_w2"],
        "L0_conv_rpe_b2": _L0_conv_in["rpe_b2"],
        "L0_conv_rpe_w3": _L0_conv_in["rpe_w3"],
        "L0_conv_rpe_b3": _L0_conv_in["rpe_b3"],
        "L0_conv_rpe_out_w": _L0_conv_in["rpe_out_w"],
        "L0_conv_rpe_out_b": _L0_conv_in["rpe_out_b"],
        "L0_ffn_fc1_w": _L0_ffn_in["fc1_w"],
        "L0_ffn_fc1_b": _L0_ffn_in["fc1_b"],
        "L0_ffn_fc2_w": _L0_ffn_in["fc2_w"],
        "L0_ffn_fc2_b": _L0_ffn_in["fc2_b"],
    }

def reference(x, L0_conv_Wu, L0_conv_bu, L0_conv_Wv, L0_conv_bv, L0_conv_Wo, L0_conv_bo, L0_conv_rpe_pos_w, L0_conv_rpe_pos_b, L0_conv_rpe_w1, L0_conv_rpe_b1, L0_conv_rpe_w2, L0_conv_rpe_b2, L0_conv_rpe_w3, L0_conv_rpe_b3, L0_conv_rpe_out_w, L0_conv_rpe_out_b, L0_ffn_fc1_w, L0_ffn_fc1_b, L0_ffn_fc2_w, L0_ffn_fc2_b):
    import jax
    import jax.numpy as jnp
    def _L0_conv_ref(x, H, W, Wu, bu, Wv, bv, Wo, bo, rpe_pos_w, rpe_pos_b, rpe_w1, rpe_b1, rpe_w2, rpe_b2, rpe_w3, rpe_b3, rpe_out_w, rpe_out_b):
        import jax, jax.numpy as jnp
        import numpy as np
        EPS = 1e-06
        NUM_HEADS = 8
        GAMMA = 0.999

        def simple_rms_norm(x):
            return x * jax.lax.rsqrt(jnp.mean(x * x, axis=-1, keepdims=True) + EPS)

        def gtu2d_forward(x, Wu, bu, Wv, bv, Wo, bo, rpe_pos_w, rpe_pos_b, rpe_w1, rpe_b1, rpe_w2, rpe_b2, rpe_w3, rpe_b3, rpe_out_w, rpe_out_b):
            B, n, m, E = x.shape
            d1 = Wu.shape[1]
            hd = d1 // NUM_HEADS
            u = jax.nn.silu(x @ Wu + bu)
            v = jax.nn.silu(x @ Wv + bv)
            v = v.reshape(B, n, m, NUM_HEADS, hd).transpose(0, 3, 1, 2, 4)
            ii = jnp.arange(-(n - 1), n, dtype=jnp.float32)
            jj = jnp.arange(-(m - 1), m, dtype=jnp.float32)
            pos = jnp.stack(jnp.meshgrid(ii, jj, indexing='ij'), axis=-1)
            r = pos @ rpe_pos_w + rpe_pos_b
            for w, b in ((rpe_w1, rpe_b1), (rpe_w2, rpe_b2), (rpe_w3, rpe_b3)):
                r = jax.nn.relu(simple_rms_norm(r)) @ w + b
            r = jax.nn.relu(simple_rms_norm(r)) @ rpe_out_w + rpe_out_b
            a = r.reshape(2 * n - 1, 2 * m - 1, NUM_HEADS, hd).transpose(2, 0, 1, 3)
            dist = jnp.abs(pos[..., 0]) + jnp.abs(pos[..., 1])
            a = a * (GAMMA ** dist)[None, :, :, None]
            t = jnp.zeros((NUM_HEADS, 2 * n, 2 * m, hd), a.dtype)
            t = t.at[:, :n, :m].set(a[:, n - 1:, m - 1:])
            t = t.at[:, n + 1:, :m].set(a[:, :n - 1, m - 1:])
            t = t.at[:, :n, m + 1:].set(a[:, n - 1:, :m - 1])
            t = t.at[:, n + 1:, m + 1:].set(a[:, :n - 1, :m - 1])
            xf = jnp.fft.rfft2(v, s=(2 * n, 2 * m), axes=(2, 3))
            tf = jnp.fft.rfft2(t, s=(2 * n, 2 * m), axes=(1, 2))
            y = jnp.fft.irfft2(xf * tf[None], s=(2 * n, 2 * m), axes=(2, 3))[:, :, :n, :m, :]
            y = y.transpose(0, 2, 3, 1, 4).reshape(B, n, m, d1)
            return u * y @ Wo + bo
        return gtu2d_forward(x, Wu, bu, Wv, bv, Wo, bo, rpe_pos_w, rpe_pos_b, rpe_w1, rpe_b1, rpe_w2, rpe_b2, rpe_w3, rpe_b3, rpe_out_w, rpe_out_b)

    def _L0_ffn_ref(x, fc1_w, fc1_b, fc2_w, fc2_b):
        import jax, jax.numpy as jnp
        import numpy as np

        def _haar_dwt2(x):
            a = x[:, ::2, ::2]
            b = x[:, ::2, 1::2]
            c = x[:, 1::2, ::2]
            d = x[:, 1::2, 1::2]
            ll = (a + b + c + d) * 0.5
            lh = (a + b - c - d) * 0.5
            hl = (a - b + c - d) * 0.5
            hh = (a - b - c + d) * 0.5
            return (ll, lh, hl, hh)

        def _haar_idwt2(ll, lh, hl, hh):
            a = (ll + lh + hl + hh) * 0.5
            b = (ll + lh - hl - hh) * 0.5
            c = (ll - lh + hl - hh) * 0.5
            d = (ll - lh - hl + hh) * 0.5
            B, H2, W2 = ll.shape
            out = jnp.zeros((B, 2 * H2, 2 * W2), ll.dtype)
            out = out.at[:, ::2, ::2].set(a)
            out = out.at[:, ::2, 1::2].set(b)
            out = out.at[:, 1::2, ::2].set(c)
            out = out.at[:, 1::2, 1::2].set(d)
            return out

        def _interp_linear_last(x, m):
            n = x.shape[-1]
            pos = jnp.linspace(0.0, 1.0, m, dtype=x.dtype) * (n - 1)
            i0 = jnp.clip(jnp.floor(pos).astype(jnp.int32), 0, n - 2)
            w = pos - i0.astype(x.dtype)
            return x[..., i0] * (1.0 - w) + x[..., i0 + 1] * w
        b, f, c = x.shape
        ll, lh, hl, hh = _haar_dwt2(x)
        ll_up = _interp_linear_last(ll, c)
        h = jax.nn.gelu(jnp.einsum('bfc,hc->bfh', ll_up, fc1_w) + fc1_b, approximate=False)
        ll_new = jnp.einsum('bfh,oh->bfo', h, fc2_w) + fc2_b
        return _haar_idwt2(ll_new, lh, hl, hh)

    def _gn(v, G=32, eps=1e-5):
        B_, H_, W_, C_ = v.shape
        g = v.reshape(B_, H_, W_, G, C_ // G)
        m = jnp.mean(g, axis=(1, 2, 4), keepdims=True)
        s = jnp.var(g, axis=(1, 2, 4), keepdims=True)
        return ((g - m) / jnp.sqrt(s + eps)).reshape(v.shape)

    def _ln_c(v, eps=1e-6):
        m = jnp.mean(v, axis=-1, keepdims=True)
        s = jnp.var(v, axis=-1, keepdims=True)
        return (v - m) / jnp.sqrt(s + eps)

    def _ln_t(v, eps=1e-5):
        m = jnp.mean(v, axis=-1, keepdims=True)
        s = jnp.var(v, axis=-1, keepdims=True)
        return (v - m) / jnp.sqrt(s + eps)

    def _to_tokens(v):
        B_, H_, W_, C_ = v.shape
        return v.reshape(B_, H_ * W_, C_)
    def _from_tokens(t, like):
        return t.reshape(like.shape)

    x = x + _L0_conv_ref(_ln_c(x), 14, 14, L0_conv_Wu, L0_conv_bu, L0_conv_Wv, L0_conv_bv, L0_conv_Wo, L0_conv_bo, L0_conv_rpe_pos_w, L0_conv_rpe_pos_b, L0_conv_rpe_w1, L0_conv_rpe_b1, L0_conv_rpe_w2, L0_conv_rpe_b2, L0_conv_rpe_w3, L0_conv_rpe_b3, L0_conv_rpe_out_w, L0_conv_rpe_out_b)
    t = _to_tokens(x)
    t = t + _L0_ffn_ref(_ln_t(t), L0_ffn_fc1_w, L0_ffn_fc1_b, L0_ffn_fc2_w, L0_ffn_fc2_b)
    x = _from_tokens(t, x)
    return x


_drawn_inputs = setup_inputs


def setup_inputs(seed=0):
    import zlib

    import numpy as np

    out = dict(_drawn_inputs(seed))
    spreads = {'L0_conv_bu': (0.0, 0.1),
     'L0_conv_bv': (0.0, 0.1),
     'L0_conv_bo': (0.0, 0.1),
     'L0_conv_rpe_pos_b': (0.0, 0.1),
     'L0_conv_rpe_b1': (0.0, 0.1),
     'L0_conv_rpe_b2': (0.0, 0.1),
     'L0_conv_rpe_b3': (0.0, 0.1),
     'L0_conv_rpe_out_b': (0.0, 0.1),
     'L0_ffn_fc1_b': (0.0, 0.664),
     'L0_ffn_fc2_b': (0.0, 0.327)}
    factors = {}
    for name, (base, spread) in spreads.items():
        noise = np.random.default_rng([zlib.crc32(name.encode()), seed]).standard_normal(out[name].shape)
        drawn = base * np.exp(spread * noise) if base else spread * noise
        out[name] = jnp.asarray(drawn.astype(out[name].dtype))
    for name, factor in factors.items():
        out[name] = (out[name] * factor).astype(out[name].dtype)
    return out
```

```python
from contextlib import ExitStack

import numpy as np

import concourse.bass as bass
from concourse import mybir

F32 = mybir.dt.float32
F32R = mybir.dt.float32r
ALU = mybir.AluOpType
ACT = mybir.ActivationFunctionType

P = 128
IMAGES, SIDE = 64, 14
POS = SIDE * SIDE
HALF = POS // 2
ROWS_HALF = SIDE // 2
TOKENS = IMAGES * POS
TILES = TOKENS // P
E = 512
EC = E // P
D = 1024
DC = D // P
HID = 2048
HC = HID // P
LL = E // 2
LC = LL // P
REL = 2 * SIDE - 1
NREL = REL * REL
CC = 16
CHUNKS = D // CC
VC = P
TROWS = ROWS_HALF + SIDE
GT = 4
GROUPS = -(-TILES // GT)
LN1_EPS, LN2_EPS, RMS_EPS = 1e-6, 1e-5, 1e-6


class Env:
    pass


def rel_mlp(nc, d, env):
    NH = [(0, 365), (365, NREL)]
    TP = 4 * REL
    OT = [(m, min(m + TP, NREL)) for m in range(0, NREL, TP)]
    L = 4
    with ExitStack() as ctx:
        sb = lambda n, s, t=F32: ctx.enter_context(nc.sbuf_tensor(n, s, t))
        sem = lambda n: ctx.enter_context(nc.semaphore(n))
        pos = sb("pos", [2, NREL])
        pos_w = sb("pos_w", [2, E])
        bias = sb("mlp_bias", [P, L, EC])
        gamma = sb("gamma", [P, len(OT)])
        bout = sb("bout", [P, D])
        w = sb("mlp_w", [P, 3, EC, E])
        wout = sb("mlp_wout", [P, EC, D])
        ones = sb("ones", [P, P])
        X = sb("mlp_x", [P, EC, NREL])
        SQ = sb("mlp_sq", [P, EC, NREL])
        H = sb("mlp_h", [P, EC, NREL])
        S = sb("mlp_s", [P, NREL])
        S2 = sb("mlp_s2", [P, NREL])
        banks = [ctx.enter_context(nc.psum_tensor(f"mlp_ps{i}", [P, 512], F32)) for i in range(8)]
        loaded, wloaded, ones_set = sem("mlp_loaded"), sem("mlp_wloaded"), sem("ones_set")
        prod, biased, squared, summed = sem("mlp_prod"), sem("mlp_biased"), sem("mlp_squared"), sem("mlp_summed")
        meaned, rooted, hready, chain = sem("mlp_meaned"), sem("mlp_rooted"), sem("mlp_hready"), sem("mlp_chain")
        aprod, aready = sem("mlp_aprod"), sem("mlp_aready")
        block = ctx.enter_context(nc.Block())
        half = lambda t, n: t[:, NH[n][0]:NH[n][1]]
        width = lambda n: NH[n][1] - NH[n][0]

        @block.sync
        def _(sp):
            sp.dma_start(pos[:], d["rel_pos"]).then_inc(loaded, 16)
            sp.dma_start(pos_w[:], d["L0_conv_rpe_pos_w"]).then_inc(loaded, 16)
            sp.dma_start(bias[:], d["mlp_bias"]).then_inc(loaded, 16)
            sp.dma_start(gamma[:], d["rel_gamma"]).then_inc(loaded, 16)
            b = d["L0_conv_rpe_out_b"]
            sp.dma_start(bout[:], bass.AP(b.tensor, 0, [[0, P], [1, D]])).then_inc(loaded, 16)
            for i in range(3):
                sp.dma_start(w[:, i], d[f"L0_conv_rpe_w{i + 1}"].rearrange("(k p) n -> p k n", p=P)).then_inc(wloaded, 16)
            sp.dma_start(wout[:], d["L0_conv_rpe_out_w"].rearrange("(k p) n -> p k n", p=P)).then_inc(wloaded, 16)
            for t, (m0, m1) in enumerate(OT):
                sp.wait_ge(aready, t + 1)
                dst = bass.AP(env.a_dram.tensor, m0 * CC, [[CC, m1 - m0], [NREL * CC, CHUNKS], [1, CC]])
                sp.dma_start(dst, env.a_tile[0:m1 - m0, t, :].rearrange("p (k c) -> p k c", c=CC)).then_inc(env.a_stored, 16)

        @block.tensor
        def _(pe):
            pe.wait_ge(loaded, 80)
            for l in range(L):
                if l == 1:
                    pe.wait_ge(wloaded, 64)
                if l:
                    pe.wait_ge(hready, EC * l)
                for m in range(EC):
                    for n in range(2):
                        use = EC * l + m
                        if use >= 3:
                            pe.wait_ge(biased, 2 * (use - 3) + n + 1)
                        out = banks[2 * (use % 3) + n][:, 0:width(n)]
                        if l == 0:
                            mm = nc.tensor.matmul(out, pos_w[:, m * P:(m + 1) * P], half(pos, n), start=True, stop=True)
                        else:
                            for k in range(EC):
                                mm = nc.tensor.matmul(out, w[:, l - 1, k, m * P:(m + 1) * P], half(H[:, k], n),
                                                      start=(k == 0), stop=(k == EC - 1))
                        mm.then_inc(prod, 1)
                if l == 0:
                    pe.wait_ge(ones_set, 1)
                for k in range(EC):
                    pe.wait_ge(squared, EC * l + k + 1)
                    for n in range(2):
                        if k == 0 and l:
                            pe.wait_ge(meaned, 2 * l)
                        mm = nc.tensor.matmul(banks[6 + n][:, 0:width(n)], ones[:], half(SQ[:, k], n),
                                              start=(k == 0), stop=(k == EC - 1))
                mm.then_inc(summed, 1)
            pe.wait_ge(hready, EC * L)
            pe.wait_ge(biased, 2 * EC * L)
            for t, (m0, m1) in enumerate(OT):
                for n in range(2):
                    if t >= 3:
                        pe.wait_ge(aready, t - 2)
                    for k in range(EC):
                        mm = nc.tensor.matmul(banks[2 * (t % 3) + n][0:m1 - m0, :], H[:, k, m0:m1],
                                              wout[:, k, n * 512:(n + 1) * 512], start=(k == 0), stop=(k == EC - 1))
                mm.then_inc(aprod, 1)

        @block.scalar
        def _(act):
            for l in range(L):
                for k in range(EC):
                    act.wait_ge(biased, 2 * (EC * l + k) + 2)
                    if l:
                        act.wait_ge(summed, l)
                    nc.scalar.activation(SQ[:, k], X[:, k], ACT.Square).then_inc(squared, 1)
                act.wait_ge(meaned, 2 * (l + 1))
                nc.scalar.activation(S2[:], S[:], ACT.Sqrt).then_inc(rooted, 1)

        @block.vector
        def _(dve):
            steps = [0]

            def link(ins):
                steps[0] += 1
                ins.then_inc(chain, 1)
                dve.wait_ge(chain, steps[0])

            nc.vector.memset(ones[:], 1.0).then_inc(ones_set, 1)
            dve.wait_ge(loaded, 80)
            for l in range(L):
                for m in range(EC):
                    for n in range(2):
                        use = EC * l + m
                        dve.wait_ge(prod, 2 * use + n + 1)
                        nc.vector.tensor_scalar(half(X[:, m], n), banks[2 * (use % 3) + n][:, 0:width(n)],
                                                bias[:, l, m:m + 1], None, ALU.add).then_inc(biased, 1)
                dve.wait_ge(summed, l + 1)
                if l:
                    dve.wait_ge(rooted, l)
                for n in range(2):
                    nc.vector.tensor_scalar(half(S, n), banks[6 + n][:, 0:width(n)], 1.0 / E, RMS_EPS,
                                            ALU.mult, ALU.add).then_inc(meaned, 1)
                dve.wait_ge(rooted, l + 1)
                link(nc.vector.reciprocal(S[:], S2[:]))
                for k in range(EC):
                    nc.vector.scalar_tensor_tensor(out=H[:, k], in0=X[:, k], scalar=0.0, in1=S[:],
                                                   op0=ALU.max, op1=ALU.mult).then_inc(hready, 1)
            for t, (m0, m1) in enumerate(OT):
                dve.wait_ge(aprod, t + 1)
                a = env.a_tile[0:m1 - m0, t, :]
                for n in range(2):
                    c = slice(n * 512, (n + 1) * 512)
                    link(nc.vector.tensor_tensor(a[:, c], banks[2 * (t % 3) + n][0:m1 - m0, :], bout[0:m1 - m0, c], ALU.add))
                nc.vector.tensor_scalar(a, a, gamma[0:m1 - m0, t:t + 1], None, ALU.mult).then_inc(aready, 1)


def values(nc, d, env):
    with ExitStack() as ctx:
        sb = lambda n, s, t=F32: ctx.enter_context(nc.sbuf_tensor(n, s, t))
        sem = lambda n: ctx.enter_context(nc.semaphore(n))
        wv = sb("wv", [P, EC, D])
        wvh, wvl = sb("wvh", [P, EC, D], F32R), sb("wvl", [P, EC, D], F32R)
        bvb = sb("bvb", [P, D])
        ident = sb("identA", [P, P])
        minus_half = sb("minus_halfA", [P, 1])
        step_in = sb("step_inA", [P, 1])
        x = [sb(f"xA{i}", [P, E]) for i in range(2)]
        xn = [sb(f"xnA{i}", [P, E]) for i in range(2)]
        xth = [sb(f"xthA{i}", [P, E], F32R) for i in range(2)]
        xtl = [sb(f"xtlA{i}", [P, E], F32R) for i in range(2)]
        v = [sb(f"vA{i}", [P, D]) for i in range(2)]
        stat = [sb(f"statA{i}", [P, 6]) for i in range(2)]
        mv = [sb(f"mvA{i}", [P, 2]) for i in range(2)]
        var = [sb(f"varA{i}", [P, 1]) for i in range(2)]
        rstd = [sb(f"rstdA{i}", [P, 1]) for i in range(2)]
        psT = [ctx.enter_context(nc.psum_tensor(f"psTA{i}", [P, E], F32)) for i in range(2)]
        psV = [[ctx.enter_context(nc.psum_tensor(f"psVA{i}{n}", [P, 512], F32)) for n in range(2)] for i in range(2)]
        w_loaded, w_split, const_set = sem("wv_loaded"), sem("wv_split"), sem("constA")
        x_loaded = [sem(f"xA_loaded{i}") for i in range(2)]
        v_stored = [sem(f"vA_stored{i}") for i in range(2)]
        chain, mean_ready, var_ready, rstd_ready = sem("chainA"), sem("meanA"), sem("varA"), sem("rstdA")
        normed, turned, hi_ready, lo_ready = sem("normedA"), sem("turnedA"), sem("hiA"), sem("loA")
        v_prod, v_pre, v_act = sem("v_prod"), sem("v_pre"), sem("v_act")
        block = ctx.enter_context(nc.Block())
        PAIRS = TILES // 2

        def both(eng, step):
            for s in range(2):
                step(0, s, True)
            with eng.Fori(1, PAIRS) as j:
                for s in range(2):
                    step(j, s, False)

        @block.sync
        def _(sp):
            sp.dma_start(wv[:], d["L0_conv_Wv"].rearrange("(k p) n -> p k n", p=P)).then_inc(w_loaded, 16)
            b = d["L0_conv_bv"]
            sp.dma_start(bvb[:], bass.AP(b.tensor, 0, [[0, P], [1, D]])).then_inc(w_loaded, 16)
            sp.dma_start(ident[:], d["ident"]).then_inc(w_loaded, 16)

            def load(j, s, first):
                if not first:
                    sp.wait_ge(normed, 2 * j + s - 1)
                sp.dma_start(x[s][:], d["x"][bass.ds((2 * j + s) * P, P), :]).then_inc(x_loaded[s], 16)

            both(sp, load)
            sp.wait_ge(env.a_stored, 16 * env.a_tiles)

        @block.gpsimd
        def _(pool):
            nc.gpsimd.memset(minus_half[:], -0.5).then_inc(const_set, 1)
            pool.wait_ge(const_set, 1)

            def root(j, s, first):
                pool.wait_ge(var_ready, 2 * j + s + 1)
                if not first:
                    pool.wait_ge(normed, 2 * j + s - 1)
                nc.gpsimd.tensor_tensor(rstd[s][:], var[s][:], minus_half[:], ALU.pow).then_inc(rstd_ready, 1)

            both(pool, root)

        @block.vector
        def _(dve):
            dve.wait_ge(w_loaded, 48)
            nc.vector.tensor_copy(wvh[:], wv[:]).then_inc(w_split, 1)
            dve.wait_ge(w_split, 1)
            nc.vector.tensor_tensor(wvl[:], wv[:], wvh[:].bitcast(F32), ALU.subtract).then_inc(w_split, 1)

            def norm(j, s, first):
                t = 2 * j + s
                dve.wait_ge(x_loaded[s], 16 * (j + 1) if not first else 16)
                nc.vector.bn_stats(stat[s][:], x[s][:]).then_inc(chain, 1)
                dve.wait_ge(chain, t + 1)
                nc.vector.memset(step_in[:], 0.0)
                nc.vector.bn_aggr(mv[s][:], stat[s][:]).then_inc(mean_ready, 1)
                dve.wait_ge(mean_ready, t + 1)
                nc.vector.tensor_scalar(var[s][:], mv[s][:, 1:2], LN1_EPS, None, ALU.add).then_inc(var_ready, 1)
                dve.wait_ge(rstd_ready, t + 1)
                if not first:
                    dve.wait_ge(turned, t - 1)
                nc.vector.tensor_scalar(xn[s][:], x[s][:], mv[s][:, 0:1], rstd[s][:], ALU.subtract, ALU.mult).then_inc(normed, 1)

            def low(j, s, first):
                t = 2 * j + s
                dve.wait_ge(hi_ready, t + 1)
                if not first:
                    dve.wait_ge(v_prod, t - 1)
                nc.vector.tensor_tensor(xtl[s][:], psT[s][:], xth[s][:].bitcast(F32), ALU.subtract).then_inc(lo_ready, 1)

            def bias(j, s, first):
                t = 2 * j + s
                dve.wait_ge(v_prod, t + 1)
                if not first:
                    dve.wait_ge(v_stored[s], 16 * j)
                for n in range(2):
                    c = slice(n * 512, (n + 1) * 512)
                    nc.vector.tensor_tensor(v[s][:, c], psV[s][n][:], bvb[:, c], ALU.add).then_inc(v_pre, 1)

            norm(0, 0, True)
            low(0, 0, True)
            norm(0, 1, True)
            low(0, 1, True)
            norm(1, 0, False)
            bias(0, 0, True)
            low(1, 0, False)
            norm(1, 1, False)
            bias(0, 1, True)
            low(1, 1, False)
            with dve.Fori(1, PAIRS - 1) as j:
                for s in range(2):
                    norm(j + 1, s, False)
                    bias(j, s, False)
                    low(j + 1, s, False)
            for s in range(2):
                bias(PAIRS - 1, s, False)

        @block.tensor
        def _(pe):
            pe.wait_ge(w_split, 2)

            def turn(j, s, first):
                t = 2 * j + s
                pe.wait_ge(normed, t + 1)
                if not first:
                    pe.wait_ge(lo_ready, t - 1)
                for k in range(EC):
                    mm = nc.tensor.transpose(psT[s][:, k * P:(k + 1) * P], xn[s][:, k * P:(k + 1) * P], ident[:])
                mm.then_inc(turned, 1)

            def project(j, s, first):
                t = 2 * j + s
                pe.wait_ge(lo_ready, t + 1)
                if not first:
                    pe.wait_ge(v_pre, 2 * (t - 1))
                parts = [(xth[s], wvh), (xth[s], wvl), (xtl[s], wvh)]
                for n in range(2):
                    for k in range(EC):
                        for i, (a, b) in enumerate(parts):
                            mm = nc.tensor.matmul(psV[s][n][:], a[:, k * P:(k + 1) * P], b[:, k, n * 512:(n + 1) * 512],
                                                  start=(k == 0 and i == 0), stop=(k == EC - 1 and i == 2))
                mm.then_inc(v_prod, 1)

            turn(0, 0, True)
            turn(0, 1, True)
            project(0, 0, True)
            turn(1, 0, False)
            project(0, 1, True)
            turn(1, 1, False)
            with pe.Fori(1, PAIRS - 1) as j:
                for s in range(2):
                    project(j, s, False)
                    turn(j + 1, s, False)
            for s in range(2):
                project(PAIRS - 1, s, False)

        @block.scalar
        def _(act):
            def high(j, s, first):
                t = 2 * j + s
                act.wait_ge(turned, t + 1)
                if not first:
                    act.wait_ge(v_prod, t - 1)
                nc.scalar.copy(xth[s][:], psT[s][:]).then_inc(hi_ready, 1)

            def silu(j, s, first):
                t = 2 * j + s
                act.wait_ge(v_pre, 2 * (t + 1))
                nc.scalar.activation(v[s][:], v[s][:], ACT.Silu).then_inc(v_act, 1)
                act.wait_ge(v_act, t + 1)
                act.dma_start(env.v_dram[bass.ds(t * P, P), :], v[s][:]).then_inc(v_stored[s], 16)

            high(0, 0, True)
            high(0, 1, True)
            with act.Fori(1, PAIRS) as j:
                for s in range(2):
                    high(j, s, False)
                    silu(j - 1, s, False)
            for s in range(2):
                silu(PAIRS - 1, s, False)
            for s in range(2):
                act.wait_ge(v_stored[s], 16 * PAIRS)


def convolve(nc, d, env):
    VCH = D // VC
    TPV = VC // CC
    HQ = CC // 2
    BANKS = HQ // 2
    PIECES = 4
    IP = IMAGES // PIECES
    with ExitStack() as ctx:
        sb = lambda n, s, t=F32: ctx.enter_context(nc.sbuf_tensor(n, s, t))
        sem = lambda n: ctx.enter_context(nc.semaphore(n))
        v = [sb(f"vB{i}", [HALF, 2, IMAGES, VC]) for i in range(2)]
        T = [sb(f"T{i}", [HALF, TROWS * SIDE, CC]) for i in range(2)]
        y = [sb(f"yB{i}", [P, HQ, POS]) for i in range(2)]
        ps = [ctx.enter_context(nc.psum_tensor(f"psB{i}", [P, 512], F32)) for i in range(2 * BANKS)]
        v_loaded = [sem(f"vB_loaded{i}") for i in range(2)]
        T_loaded = [sem(f"T_loaded{i}") for i in range(2)]
        y_stored = [sem(f"yB_stored{i}") for i in range(2)]
        bank_ready, out_dve, out_act = sem("bank_ready"), sem("y_out_dve"), sem("y_out_act")
        block = ctx.enter_context(nc.Block())

        @block.sync
        def _(sp):
            def load_v(j, s, piece):
                for kh in range(2):
                    src = env.v_dram.rearrange("(b q) c -> q b c", q=POS)[
                        kh * HALF:(kh + 1) * HALF, piece * IP:(piece + 1) * IP, bass.ds((2 * j + s) * VC, VC)]
                    sp.dma_start(v[s][:, kh, piece * IP:(piece + 1) * IP, :], src).then_inc(v_loaded[s], 16)

            def load_T(n, par):
                for p in range(ROWS_HALF):
                    src = env.a_rows[bass.ds(n, 1), p]
                    sp.dma_start(T[par][p * SIDE:(p + 1) * SIDE].rearrange("q (r s) c -> q r (s c)", r=TROWS),
                                 src.rearrange("o q r f -> (o q) r f")).then_inc(T_loaded[par], 16)

            def store_y(n, par):
                for h in range(2):
                    dst = env.y_dram.rearrange("(n h q) (b p) -> n h b q p", h=2, q=HQ, p=POS)[bass.ds(n, 1), h]
                    sp.dma_start(dst.rearrange("o b q p -> (o b) q p"), y[par][h * IMAGES:(h + 1) * IMAGES]).then_inc(y_stored[par], 16)

            def chunk(j, s, tt, first, last):
                n = 2 * TPV * j + TPV * s + tt
                if not (first and n < 2):
                    sp.wait_ge(bank_ready, BANKS * (n - 1))
                load_T(n, tt % 2)
                if 2 <= tt < 2 + PIECES:
                    if s == 0:
                        load_v(j, 1, tt - 2)
                    elif not last:
                        load_v(j + 1, 0, tt - 2)
                if not (first and n < 2):
                    sp.wait_ge(out_dve, BANKS // 2 * (n - 1))
                    sp.wait_ge(out_act, BANKS // 2 * (n - 1))
                    store_y(n - 2, tt % 2)

            for piece in range(PIECES):
                load_v(0, 0, piece)
            for s in range(2):
                for tt in range(TPV):
                    chunk(0, s, tt, True, False)
            with sp.Fori(1, VCH // 2 - 1) as j:
                for s in range(2):
                    for tt in range(TPV):
                        chunk(j, s, tt, False, False)
            for s in range(2):
                for tt in range(TPV):
                    chunk(VCH // 2 - 1, s, tt, False, True)
            for n in (CHUNKS - 2, CHUNKS - 1):
                sp.wait_ge(out_dve, BANKS // 2 * (n + 1))
                sp.wait_ge(out_act, BANKS // 2 * (n + 1))
                store_y(n, n % 2)
            for s in range(2):
                sp.wait_ge(y_stored[s], 16 * CHUNKS)

        @block.tensor
        def _(pe):
            def chunk(j, s, tt, first):
                n = 2 * TPV * j + TPV * s + tt
                par = tt % 2
                if tt == 0:
                    pe.wait_ge(v_loaded[s], 2 * PIECES * 16 * (j + 1))
                pe.wait_ge(T_loaded[par], ROWS_HALF * 16 * (TPV * j + TPV // 2 * s + tt // 2 + 1))
                for qq in range(BANKS):
                    bank = ps[par * BANKS + qq]
                    if not (first and n < 2):
                        pe.wait_ge(out_dve if qq % 2 == 0 else out_act, BANKS // 2 * (n - 2) + qq // 2 + 1)
                    for q in (2 * qq, 2 * qq + 1):
                        for kh in range(2):
                            for h in range(2):
                                c = h * HQ + q
                                mm = nc.tensor.matmul(bank[h * IMAGES:(h + 1) * IMAGES, (q % 2) * POS:(q % 2 + 1) * POS],
                                                      v[s][:, kh, :, tt * CC + c],
                                                      T[par][:, kh * HALF:kh * HALF + POS, c],
                                                      start=(kh == 0), stop=(kh == 1))
                    mm.then_inc(bank_ready, 1)

            for s in range(2):
                for tt in range(TPV):
                    chunk(0, s, tt, True)
            with pe.Fori(1, VCH // 2) as j:
                for s in range(2):
                    for tt in range(TPV):
                        chunk(j, s, tt, False)

        def evacuate(eng, copy, done, odd):
            def chunk(j, s, tt, first):
                n = 2 * TPV * j + TPV * s + tt
                par = tt % 2
                if not (first and n < 2):
                    eng.wait_ge(y_stored[par], 32 * (TPV * j + TPV // 2 * s + tt // 2))
                for qq in range(odd, BANKS, 2):
                    eng.wait_ge(bank_ready, BANKS * n + qq + 1)
                    copy(y[par][:, 2 * qq:2 * qq + 2, ::-1],
                         ps[par * BANKS + qq][:, 0:2 * POS].rearrange("p (q n) -> p q n", q=2)).then_inc(done, 1)

            for s in range(2):
                for tt in range(TPV):
                    chunk(0, s, tt, True)
            with eng.Fori(1, VCH // 2) as j:
                for s in range(2):
                    for tt in range(TPV):
                        chunk(j, s, tt, False)

        @block.vector
        def _(dve):
            evacuate(dve, nc.vector.tensor_copy, out_dve, 0)

        @block.scalar
        def _(act):
            evacuate(act, nc.scalar.copy, out_act, 1)


def split_weights(nc, d, env):
    with ExitStack() as ctx:
        sb = lambda n, s, t=F32: ctx.enter_context(nc.sbuf_tensor(n, s, t))
        sem = lambda n: ctx.enter_context(nc.semaphore(n))
        HALF_W = 2048
        stage = [sb(f"stage{i}", [P, HALF_W]) for i in range(2)]
        interp = sb("interp", [P, EC, LL])
        w1_ps = [ctx.enter_context(nc.psum_tensor(f"w1_ps{i}", [P, 512], F32)) for i in range(8)]
        staged = [sem(f"staged{i}") for i in range(2)]
        interp_loaded = sem("interp_loaded")
        hi_done, lo_done, fc1_used, w1_hi, w1_lo = sem("w_hi"), sem("w_lo"), sem("fc1_used"), sem("w1_hi_done"), sem("w1_lo_done")
        block = ctx.enter_context(nc.Block())
        fc1 = d["fc1_wT"].rearrange("(k p) n -> p k n", p=P)
        split = []
        for name, w, chunks in (("L0_conv_Wu", env.wu, EC), ("L0_conv_Wo", env.wo, DC), ("fc2_wT", env.w2, HC)):
            src = d[name].rearrange("(k p) n -> p k n", p=P)
            for i in range(2):
                k = slice(i * chunks // 2, (i + 1) * chunks // 2)
                split.append((src[:, k, :], w[0][:, k, :], w[1][:, k, :]))

        @block.sync
        def _(sp):
            sp.dma_start(interp[:], d["interpT"].rearrange("(k p) n -> p k n", p=P)).then_inc(interp_loaded, 16)
            for k in range(EC):
                if k >= 2:
                    sp.wait_ge(fc1_used, k - 1)
                sp.dma_start(stage[k % 2][:], fc1[:, k, :]).then_inc(staged[k % 2], 16)
            for i, (src, _, _) in enumerate(split):
                if i < 2:
                    sp.wait_ge(fc1_used, EC - 1 + i)
                else:
                    sp.wait_ge(lo_done, i - 1)
                n = src.shape[1]
                sp.dma_start(stage[i % 2][:].rearrange("p (k n) -> p k n", k=n), src).then_inc(staged[i % 2], 16)

        @block.tensor
        def _(pe):
            pe.wait_ge(interp_loaded, 16)
            for k in range(EC):
                pe.wait_ge(staged[k % 2], 16 * (k // 2 + 1))
                for r in range(LC):
                    for n in range(4):
                        mm = nc.tensor.matmul(w1_ps[4 * r + n][:], interp[:, k, r * P:(r + 1) * P],
                                              stage[k % 2][:, n * 512:(n + 1) * 512], start=(k == 0), stop=(k == EC - 1))
                mm.then_inc(fc1_used, 1)

        @block.scalar
        def _(act):
            act.wait_ge(fc1_used, EC)
            for r in range(LC):
                for n in range(4):
                    nc.scalar.copy(env.w1[0][:, r, n * 512:(n + 1) * 512], w1_ps[4 * r + n][:]).then_inc(w1_hi, 1)
            for i, (_, hi, _) in enumerate(split):
                act.wait_ge(staged[i % 2], 16 * (2 + i // 2 + 1))
                nc.scalar.copy(hi, stage[i % 2][:].rearrange("p (k n) -> p k n", k=hi.shape[1])).then_inc(hi_done, 1)

        @block.vector
        def _(dve):
            for r in range(LC):
                for n in range(4):
                    dve.wait_ge(w1_hi, 4 * r + n + 1)
                    c = slice(n * 512, (n + 1) * 512)
                    nc.vector.tensor_tensor(env.w1[1][:, r, c], w1_ps[4 * r + n][:], env.w1[0][:, r, c].bitcast(F32),
                                            ALU.subtract).then_inc(w1_lo, 1)
            for i, (_, hi, lo) in enumerate(split):
                dve.wait_ge(hi_done, i + 1)
                nc.vector.tensor_tensor(lo, stage[i % 2][:].rearrange("p (k n) -> p k n", k=hi.shape[1]), hi.bitcast(F32),
                                        ALU.subtract).then_inc(lo_done, 1)
            dve.wait_ge(lo_done, len(split))
            dve.wait_ge(w1_lo, 4 * LC)


def groups(nc, d, env):
    G = GT * P
    GP = G // 2
    YR, HR = 4, 3
    with ExitStack() as ctx:
        sb = lambda n, s, t=F32: ctx.enter_context(nc.sbuf_tensor(n, s, t))
        psum = lambda n: ctx.enter_context(nc.psum_tensor(n, [P, 512], F32))
        sem = lambda n: ctx.enter_context(nc.semaphore(n))
        ident, pair = sb("ident", [P, P]), sb("pair", [P, P // 2])
        spread, minus_ll = sb("spread", [P, 2 * P]), sb("minus_ll", [P, P])
        bu, b1 = sb("bu", [P, DC]), sb("b1", [P, HC])
        bo, b2 = sb("bo", [P, E]), sb("b2", [P, LL])
        minus_half = sb("minus_half", [P, GT])
        step_in, half_col, warm = sb("step_in", [P, 1]), sb("half_col", [P, 1]), sb("warm", [P, 2])
        x, xn, x1, r = (sb(n, [P, GT, E]) for n in ("x", "xn", "x1", "r"))
        s = sb("s", [P, GT, LL])
        xth, xtl = sb("xth", [P, EC, G], F32R), sb("xtl", [P, EC, G], F32R)
        y = sb("y", [P, YR, G])
        u = sb("u", [P, 2, G])
        zh, zl = sb("zh", [P, 2, G], F32R), sb("zl", [P, 2, G], F32R)
        llh, lll = sb("llh", [P, LC, GP], F32R), sb("lll", [P, LC, GP], F32R)
        hf = sb("hf", [P, 2, GP])
        hh, hl = sb("hh", [P, HR, GP], F32R), sb("hl", [P, HR, GP], F32R)
        lln = sb("lln", [P, 2, LL])
        stat1, stat2 = sb("stat1", [P, GT, 6]), sb("stat2", [P, GT, 6])
        mv1, mv2 = sb("mv1", [P, GT, 2]), sb("mv2", [P, GT, 2])
        var1, var2, rstd1, rstd2 = (sb(n, [P, GT]) for n in ("var1", "var2", "rstd1", "rstd2"))
        acc = [psum(f"acc{i}") for i in range(GT)]
        work = [psum(f"work{i}") for i in range(2)]
        ffn = [psum(f"ffn{i}") for i in range(2)]
        const_loaded, half_set, b2_halved = sem("const_loaded"), sem("half_set"), sem("b2_halved")
        x_loaded, out_stored = sem("x_loaded"), sem("out_stored")
        y_loaded = [sem(f"y_loaded{i}") for i in range(YR)]
        stats1, means1, var1_ready, rstd1_ready = sem("stats1"), sem("means1"), sem("var1_ready"), sem("rstd1_ready")
        stats2, means2, var2_ready, rstd2_ready = sem("stats2"), sem("means2"), sem("var2_ready"), sem("rstd2_ready")
        xn_ready, turned, xth_ready, xtl_ready, bo_added = (sem(n) for n in ("xn_ready", "turned", "xth_ready", "xtl_ready", "bo_added"))
        u_prod, u_ready, z_made, zh_ready, zl_ready, wo_used, acc_ready = (
            sem(n) for n in ("u_prod", "u_ready", "z_made", "zh_ready", "zl_ready", "wo_used", "acc_ready"))
        x1_ready, xn2_ready, s_ready, r_ready = (sem(n) for n in ("x1_ready", "xn2_ready", "s_ready", "r_ready"))
        ll_prod, llh_ready, lll_ready = sem("ll_prod"), sem("llh_ready"), sem("lll_ready")
        h_prod, h_act, hl_ready, h_used = sem("h_prod"), sem("h_act"), sem("hl_ready"), sem("h_used")
        lln_ready, d_prod, out_ready = sem("lln_ready"), sem("d_prod"), sem("out_ready")
        warmed, col_set = sem("warmed"), sem("col_set")
        block = ctx.enter_context(nc.Block())
        x_rows = d["x"]
        out_rows = d["out"]
        CONSTS = 8

        def tiles(g):
            return max(0, min(GT, TILES - GT * g)) if g >= 0 else 0

        def iterations(eng, step):
            for g in range(3):
                step(g, tiles(g), tiles(g - 1), tiles(g - 2), tiles(g + 1), g)
            with eng.Fori(3, GROUPS - 2) as g:
                step(g, GT, GT, GT, GT, 3)
            for g in range(GROUPS - 2, GROUPS + 2):
                step(g, tiles(g), tiles(g - 1), tiles(g - 2), tiles(g + 1), 3)

        @block.sync
        def _(sp):
            for t, name in ((ident, "ident"), (pair, "pair"), (spread, "spread"), (minus_ll, "minus_ll"), (bu, "bu"), (b1, "b1")):
                sp.dma_start(t[:], d[name]).then_inc(const_loaded, 16)
            for t, name, n in ((bo, "L0_conv_bo", E), (b2, "L0_ffn_fc2_b", LL)):
                sp.dma_start(t[:], bass.AP(d[name].tensor, 0, [[0, P], [1, n]])).then_inc(const_loaded, 16)

            def load_x(g, nt):
                src = x_rows[bass.ds(g * G, nt * P), :].rearrange("(i p) c -> p i c", p=P)
                sp.dma_start(x[:, 0:nt, :], src).then_inc(x_loaded, 16)

            def load_y(g, m, nt):
                sp.dma_start(y[:, m % YR, 0:nt * P], env.y_dram[m * P:(m + 1) * P, bass.ds(g * G, nt * P)]).then_inc(y_loaded[m % YR], 16)

            load_x(0, GT)
            for m in range(YR):
                load_y(0, m, GT)

            def step(g, cur, prev, last, nxt, age):
                if last:
                    sp.wait_ge(out_ready, GT * (g - 2) + last)
                    dst = out_rows[bass.ds((g - 2) * G, last * P), :].rearrange("(i p) c -> p i c", p=P)
                    sp.dma_start(dst, r[:, 0:last, :]).then_inc(out_stored, 16)
                if cur:
                    for m in range(YR, DC):
                        sp.wait_ge(z_made, DC * g + m - YR + 1)
                        load_y(g, m, cur)
                if nxt:
                    for m in range(YR):
                        sp.wait_ge(z_made, DC * g + m + YR + 1)
                        load_y(g + 1, m, nxt)
                    sp.wait_ge(bo_added, GT * g + cur)
                    load_x(g + 1, nxt)

            iterations(sp, step)
            sp.wait_ge(out_stored, 16 * GROUPS)

        @block.gpsimd
        def _(pool):
            nc.gpsimd.memset(minus_half[:], -0.5).then_inc(half_set, 1)
            pool.wait_ge(half_set, 1)
            pool.wait_ge(const_loaded, 16 * CONSTS)

            def first_norm(g, nt):
                pool.wait_ge(var1_ready, g + 1)
                nc.gpsimd.tensor_tensor(rstd1[:, 0:nt], var1[:, 0:nt], minus_half[:, 0:nt], ALU.pow).then_inc(rstd1_ready, 1)

            first_norm(0, GT)

            def step(g, cur, prev, last, nxt, age):
                if prev:
                    pool.wait_ge(var2_ready, g)
                    nc.gpsimd.tensor_tensor(rstd2[:, 0:prev], var2[:, 0:prev], minus_half[:, 0:prev], ALU.pow).then_inc(rstd2_ready, 1)
                for i in range(cur):
                    if i == 0:
                        pool.wait_ge(xn_ready, GT * g + cur)
                    if prev:
                        pool.wait_ge(r_ready, GT * (g - 1) + i + 1)
                    nc.gpsimd.tensor_tensor(x1[:, i, :], x[:, i, :], bo[:], ALU.add).then_inc(bo_added, 1)
                if nxt:
                    first_norm(g + 1, nxt)

            iterations(pool, step)

        @block.tensor
        def _(pe):
            def turn(g, i, age):
                pe.wait_ge(xn_ready, GT * g + i + 1)
                if age:
                    pe.wait_ge(x1_ready, GT * (g - 1) + i + 1)
                for k in range(EC):
                    mm = nc.tensor.transpose(acc[i][:, k * P:(k + 1) * P], xn[:, i, k * P:(k + 1) * P], ident[:])
                mm.then_inc(turned, 1)

            def three(out, a, b, first, last):
                for i, (p, q) in enumerate(((0, 0), (0, 1), (1, 0))):
                    mm = nc.tensor.matmul(out, a[p], b[q], start=(first and i == 0), stop=(last and i == 2))
                return mm

            def step(g, cur, prev, last, nxt, age):
                n, pairs = cur * P, prev * P // 2

                def make_u(m):
                    if m == 0:
                        pe.wait_ge(xtl_ready, GT * g + cur)
                    if m >= 2:
                        pe.wait_ge(u_ready, DC * g + m - 1)
                    elif age >= 2:
                        pe.wait_ge(h_act, 2 * HC * (g - 1))
                    for k in range(EC):
                        c = slice(m * P, (m + 1) * P)
                        mm = three(work[m % 2][:, 0:n], [w[:, k, c] for w in env.wu], [t[:, k, 0:n] for t in (xth, xtl)],
                                   k == 0, k == EC - 1)
                    mm.then_inc(u_prod, 1)

                def make_ll():
                    pe.wait_ge(s_ready, GT * (g - 1) + prev)
                    if age >= 2:
                        pe.wait_ge(out_ready, GT * (g - 1))
                    for i in range(prev):
                        for c in range(LC):
                            mm = nc.tensor.matmul(ffn[1][:, c * GP + i * P // 2:c * GP + (i + 1) * P // 2],
                                                  s[:, i, c * P:(c + 1) * P], pair[:], start=True, stop=True)
                    mm.then_inc(ll_prod, 1)

                def use_z(q):
                    pe.wait_ge(zl_ready, DC * g + q + 1)
                    for i in range(cur):
                        t = slice(i * P, (i + 1) * P)
                        mm = three(acc[i][:], [z[:, q % 2, t] for z in (zh, zl)], [w[:, q, :] for w in env.wo], q == 0, q == DC - 1)
                        if q == DC - 1:
                            mm.then_inc(acc_ready, 1)
                        elif i == cur - 1:
                            mm.then_inc(wo_used, 1)

                def make_h(m):
                    if m == 0:
                        pe.wait_ge(lll_ready, g)
                    if m >= 2:
                        pe.wait_ge(h_act, 2 * (HC * (g - 1) + m - 1))
                    elif cur:
                        pe.wait_ge(u_ready, DC * g + DC - 1 + m)
                    else:
                        pe.wait_ge(h_act, 2 * HC * (g - 1))
                    for k in range(LC):
                        c = slice(m * P, (m + 1) * P)
                        mm = three(work[m % 2][:, 0:pairs], [w[:, k, c] for w in env.w1], [t[:, k, 0:pairs] for t in (llh, lll)],
                                   k == 0, k == LC - 1)
                    mm.then_inc(h_prod, 1)

                def use_h(q):
                    pe.wait_ge(hl_ready, HC * (g - 1) + q + 1)
                    for t in range(prev // 2):
                        c = slice(t * P, (t + 1) * P)
                        mm = three(ffn[t][:, 0:LL], [h[:, q % HR, c] for h in (hh, hl)], [w[:, q, :] for w in env.w2],
                                   q == 0, q == HC - 1)
                    mm.then_inc(h_used, 1)

                def make_sum(i):
                    if i < 2:
                        pe.wait_ge(lln_ready, g - 1)
                    else:
                        pe.wait_ge(out_ready, GT * (g - 2) + i - 1)
                    out = ffn[i % 2][:, 0:LL]
                    nc.tensor.matmul(out, spread[:, (i % 2) * P:(i % 2 + 1) * P], lln[:, i // 2, :], start=True, stop=False)
                    nc.tensor.matmul(out, minus_ll[:], s[:, i, :], start=False, stop=True).then_inc(d_prod, 1)

                for m in range(DC):
                    if cur:
                        make_u(m)
                    if prev and m == DC - 1:
                        make_ll()
                    if m == 0:
                        for i in range(last):
                            make_sum(i)
                    if cur and m >= 1:
                        use_z(m - 1)
                if prev:
                    make_h(0)
                    make_h(1)
                if cur:
                    use_z(DC - 1)
                for m in range(2, HC):
                    if m >= HC - GT and m - (HC - GT) < nxt:
                        turn(g + 1, m - (HC - GT), True)
                    if prev:
                        make_h(m)
                        use_h(m - 2)
                if prev:
                    use_h(HC - 2)
                    use_h(HC - 1)

            pe.wait_ge(const_loaded, 16 * CONSTS)
            for i in range(GT):
                turn(0, i, False)
            iterations(pe, step)

        @block.scalar
        def _(act):
            act.wait_ge(const_loaded, 16 * CONSTS)
            act.wait_ge(col_set, 1)

            def high(g, i):
                act.wait_ge(turned, GT * g + i + 1)
                nc.scalar.copy(xth[:, :, i * P:(i + 1) * P], acc[i][:].rearrange("p (k t) -> p k t", k=EC)).then_inc(xth_ready, 1)

            for i in range(GT):
                high(0, i)

            def high_ll(g, pairs):
                act.wait_ge(ll_prod, g)
                nc.scalar.copy(llh[:, :, 0:pairs], ffn[1][:].rearrange("p (c t) -> p c t", c=LC)[:, :, 0:pairs]).then_inc(llh_ready, 1)

            def step(g, cur, prev, last, nxt, age):
                n, pairs = cur * P, prev * P // 2
                if cur:
                    for m in range(DC):
                        act.wait_ge(u_prod, DC * g + m + 1)
                        if age or m >= 2:
                            act.wait_ge(zl_ready, DC * g + m - 1)
                        nc.scalar.activation(u[:, m % 2, 0:n], work[m % 2][:, 0:n], ACT.Silu, bias=bu[:, m:m + 1]).then_inc(u_ready, 1)
                if prev:
                    high_ll(g, pairs)
                    nc.scalar.activation(warm[:, 1:2], half_col[:], ACT.Gelu).then_inc(warmed, 1)
                for m in range(HC):
                    if m >= HC - GT and m - (HC - GT) < nxt:
                        high(g + 1, m - (HC - GT))
                    if prev:
                        act.wait_ge(h_prod, HC * (g - 1) + m + 1)
                        if age >= 2 or m >= 2:
                            act.wait_ge(hl_ready, HC * (g - 1) + m - 1)
                        if age >= 2 or m >= HR:
                            act.wait_ge(h_used, HC * (g - 1) + m - HR + 1)
                        for dst in (hf[:, m % 2, 0:pairs], hh[:, m % HR, 0:pairs]):
                            nc.scalar.activation(dst, work[m % 2][:, 0:pairs], ACT.Gelu, bias=b1[:, m:m + 1]).then_inc(h_act, 1)
                if nxt:
                    nc.scalar.activation(warm[:, 0:1], half_col[:], ACT.Silu).then_inc(warmed, 1)

            iterations(act, step)

        @block.vector
        def _(dve):
            dve.wait_ge(const_loaded, 16 * CONSTS)
            nc.vector.memset(half_col[:], 0.5).then_inc(col_set, 1)
            nc.vector.tensor_scalar(b2[:], b2[:], 0.5, None, ALU.mult).then_inc(b2_halved, 1)
            dve.wait_ge(b2_halved, 1)

            def statistics(g, lo, hi, src, stat, done):
                for i in range(lo, hi):
                    nc.vector.bn_stats(stat[:, i, :], src[:, i, :]).then_inc(done, 1)

            def variances(g, nt, stat, stats, mv, means, var, eps, done):
                dve.wait_ge(stats, GT * g + nt)
                nc.vector.memset(step_in[:], 0.0)
                for i in range(nt):
                    nc.vector.bn_aggr(mv[:, i, :], stat[:, i, :]).then_inc(means, 1)
                dve.wait_ge(means, GT * g + nt)
                nc.vector.tensor_scalar(var[:, 0:nt], mv[:, 0:nt, 1], eps, None, ALU.add).then_inc(done, 1)

            def norm(i):
                nc.vector.tensor_scalar(xn[:, i, :], x[:, i, :], mv1[:, i, 0:1], rstd1[:, i:i + 1],
                                        ALU.subtract, ALU.mult).then_inc(xn_ready, 1)

            def low(g, i):
                dve.wait_ge(xth_ready, GT * g + i + 1)
                t = slice(i * P, (i + 1) * P)
                nc.vector.tensor_tensor(xtl[:, :, t], acc[i][:].rearrange("p (k t) -> p k t", k=EC),
                                        xth[:, :, t].bitcast(F32), ALU.subtract).then_inc(xtl_ready, 1)

            def second_norm(g, i, age):
                if i == 0:
                    dve.wait_ge(rstd2_ready, g + 1)
                    if age >= 2:
                        dve.wait_ge(out_stored, 16 * g)
                nc.vector.tensor_scalar(r[:, i, :], x1[:, i, :], mv2[:, i, 0:1], rstd2[:, i:i + 1],
                                        ALU.subtract, ALU.mult).then_inc(xn2_ready, 1)
                dve.wait_ge(xn2_ready, GT * g + i + 1)
                even_odd = r[:, i, :].rearrange("p (c e) -> p c e", e=2)
                nc.vector.tensor_tensor(s[:, i, :], even_odd[:, :, 0], even_odd[:, :, 1], ALU.add).then_inc(s_ready, 1)
                dve.wait_ge(s_ready, GT * g + i + 1)
                nc.vector.tensor_tensor(r[:, i, :], r[:, i, :], x1[:, i, :], ALU.add).then_inc(r_ready, 1)

            dve.wait_ge(x_loaded, 16)
            statistics(0, 0, GT, x, stat1, stats1)
            variances(0, GT, stat1, stats1, mv1, means1, var1, LN1_EPS, var1_ready)
            dve.wait_ge(rstd1_ready, 1)
            for i in range(GT):
                norm(i)
            for i in range(GT):
                low(0, i)

            def next_norm(g, nt, stage):
                if stage in (0, 1):
                    if stage == 0:
                        dve.wait_ge(x_loaded, 16 * (g + 1))
                    statistics(g, 2 * stage, min(2 * stage + 2, nt), x, stat1, stats1)
                elif stage == 2:
                    variances(g, nt, stat1, stats1, mv1, means1, var1, LN1_EPS, var1_ready)
                else:
                    if stage == 3:
                        dve.wait_ge(rstd1_ready, g + 1)
                        dve.wait_ge(turned, GT * g)
                    for i in range(2 * (stage - 3), min(2 * (stage - 3) + 2, nt)):
                        norm(i)

            def first_sum(g, i):
                dve.wait_ge(acc_ready, GT * g + i + 1)
                dve.wait_ge(bo_added, GT * g + i + 1)
                nc.vector.tensor_tensor(x1[:, i, :], acc[i][:], x1[:, i, :], ALU.add).then_inc(x1_ready, 1)

            NORM_AT = (4, 5, 6, 8, 9)

            def add_sum(g, i):
                dve.wait_ge(d_prod, GT * g + i + 1)
                four = r[:, i, :].rearrange("p (c e) -> p c e", e=2)
                add = ffn[i % 2][:, 0:LL].unsqueeze(2).broadcast_to([P, LL, 2])
                nc.vector.tensor_tensor(four, four, add, ALU.add).then_inc(out_ready, 1)

            def step(g, cur, prev, last, nxt, age):
                n, pairs = cur * P, prev * P // 2
                for m in range(DC):
                    if m < 2 and last:
                        if m == 0:
                            dve.wait_ge(r_ready, GT * (g - 2) + last)
                            for i in range(min(2, last)):
                                add_sum(g - 2, i)
                        else:
                            for i in range(2, last):
                                add_sum(g - 2, i)
                    if cur:
                        dve.wait_ge(u_ready, DC * g + m + 1)
                        dve.wait_ge(y_loaded[m % YR], 16 * (DC // YR * g + m // YR + 1))
                        z = u[:, m % 2, 0:n]
                        nc.vector.tensor_tensor(z, z, y[:, m % YR, 0:n], ALU.mult).then_inc(z_made, 1)
                        dve.wait_ge(z_made, DC * g + m + 1)
                        if m >= 2:
                            dve.wait_ge(wo_used, (DC - 1) * g + m - 1)
                        elif age:
                            dve.wait_ge(acc_ready, GT * g)
                        nc.vector.tensor_copy(zh[:, m % 2, 0:n], z).then_inc(zh_ready, 1)
                        dve.wait_ge(zh_ready, DC * g + m + 1)
                        nc.vector.tensor_tensor(zl[:, m % 2, 0:n], z, zh[:, m % 2, 0:n].bitcast(F32), ALU.subtract).then_inc(zl_ready, 1)
                    if prev:
                        if 0 < m < 3:
                            dve.wait_ge(x1_ready, GT * (g - 1) + prev)
                            statistics(g - 1, 2 * m - 2, min(2 * m, prev), x1, stat2, stats2)
                            if m == 2:
                                variances(g - 1, prev, stat2, stats2, mv2, means2, var2, LN2_EPS, var2_ready)
                        elif 3 <= m < 3 + prev:
                            second_norm(g - 1, m - 3, age)
                        if m == DC - 1:
                            dve.wait_ge(llh_ready, g)
                            nc.vector.tensor_tensor(lll[:, :, 0:pairs], ffn[1][:].rearrange("p (c t) -> p c t", c=LC)[:, :, 0:pairs],
                                                    llh[:, :, 0:pairs].bitcast(F32), ALU.subtract).then_inc(lll_ready, 1)
                for m in range(HC):
                    if prev:
                        dve.wait_ge(h_act, 2 * (HC * (g - 1) + m + 1))
                        if age >= 2 or m >= HR:
                            dve.wait_ge(h_used, HC * (g - 1) + m - HR + 1)
                        nc.vector.tensor_tensor(hl[:, m % HR, 0:pairs], hf[:, m % 2, 0:pairs], hh[:, m % HR, 0:pairs].bitcast(F32),
                                                ALU.subtract).then_inc(hl_ready, 1)
                    if m < cur:
                        first_sum(g, m)
                    if nxt and m in NORM_AT:
                        next_norm(g + 1, nxt, NORM_AT.index(m))
                    if m >= HC - GT and m - (HC - GT) < nxt:
                        low(g + 1, m - (HC - GT))
                if prev:
                    dve.wait_ge(h_used, HC * g)
                    for t in range(prev // 2):
                        ins = nc.vector.scalar_tensor_tensor(out=lln[:, t, :], in0=ffn[t][:, 0:LL], scalar=0.5, in1=b2[:],
                                                             op0=ALU.mult, op1=ALU.add)
                    ins.then_inc(lln_ready, 1)

            iterations(dve, step)


def metaformer(nc, d):
    env = Env()
    OT = -(-REL // 4)
    env.a_tiles = OT
    env.a_dram = nc.dram_tensor("rel_kernel", [CHUNKS, NREL, CC], F32).ap()
    env.v_dram = nc.dram_tensor("v_scratch", [TOKENS, D], F32).ap()
    env.y_dram = nc.dram_tensor("y_scratch", [D, TOKENS], F32).ap()
    env.a_rows = bass.AP(env.a_dram.tensor, 0, [[NREL * CC, CHUNKS], [REL * CC, ROWS_HALF], [CC, SIDE], [REL * CC, TROWS], [1, SIDE * CC]])
    with ExitStack() as ctx:
        env.a_stored = ctx.enter_context(nc.semaphore("a_stored"))
        with nc.sbuf_tensor("a_tile", [P, OT, D], F32) as env.a_tile:
            rel_mlp(nc, d, env)
            values(nc, d, env)
        convolve(nc, d, env)
        w = lambda n, s: [ctx.enter_context(nc.sbuf_tensor(f"{n}_{part}", s, F32R)) for part in ("hi", "lo")]
        env.wu, env.wo = w("wu", [P, EC, D]), w("wo", [P, DC, E])
        env.w1, env.w2 = w("w1", [P, LC, HID]), w("w2", [P, HC, LL])
        split_weights(nc, d, env)
        groups(nc, d, env)


def constants():
    c = {"ident": np.eye(P, dtype=np.float32)}
    tok = np.arange(P)
    c["pair"] = np.where(tok[:, None] // 2 == np.arange(P // 2), 0.5, 0.0).astype(np.float32)
    c["spread"] = np.where(np.arange(2 * P)[None, :] // 2 == tok[:, None], 1.0, 0.0).astype(np.float32)
    c["minus_ll"] = np.where(tok[:, None] // 2 == tok[None, :] // 2, -0.25, 0.0).astype(np.float32)
    at = np.linspace(0.0, 1.0, E, dtype=np.float32) * np.float32(LL - 1)
    i0 = np.clip(np.floor(at).astype(np.int32), 0, LL - 2)
    w = at - i0.astype(np.float32)
    interp = np.zeros((E, LL), np.float32)
    interp[np.arange(E), i0] = np.float32(1.0) - w
    interp[np.arange(E), i0 + 1] = w
    c["interpT"] = interp
    away = (SIDE - 1 - np.arange(REL)).astype(np.float32)
    di, dj = np.meshgrid(away, away, indexing="ij")
    c["rel_pos"] = np.stack([di.ravel(), dj.ravel()])
    g = np.float32(0.999) ** (np.abs(di) + np.abs(dj)).ravel()
    rows = 4 * REL
    gamma = np.zeros((P, -(-NREL // rows)), np.float32)
    for t in range(gamma.shape[1]):
        part = g[t * rows:(t + 1) * rows]
        gamma[:len(part), t] = part
    c["rel_gamma"] = gamma
    return c


def kernel(**inputs):
    import concourse.bacc as bacc
    from concourse.bass_utils import run_bass_kernel_spmd

    arrays = {name: np.ascontiguousarray(a) for name, a in inputs.items()}
    arrays["x"] = arrays["x"].reshape(TOKENS, E)
    cols = lambda a, n: np.ascontiguousarray(np.asarray(a).reshape(n, P).T)
    arrays["bu"] = cols(arrays.pop("L0_conv_bu"), DC)
    arrays["b1"] = cols(arrays.pop("L0_ffn_fc1_b"), HC)
    mlp_bias = [cols(arrays.pop("L0_conv_rpe_" + n), EC) for n in ("pos_b", "b1", "b2", "b3")]
    arrays["mlp_bias"] = np.ascontiguousarray(np.stack(mlp_bias, axis=1))
    arrays["fc1_wT"] = np.ascontiguousarray(arrays.pop("L0_ffn_fc1_w").T)
    arrays["fc2_wT"] = np.ascontiguousarray(arrays.pop("L0_ffn_fc2_w").T)
    arrays.update(constants())
    nc = bacc.Bacc("TRN2", target_bir_lowering=False, num_devices=1, dynamic_dma_scratch_size=1024)
    d = {n: nc.dram_tensor("in_" + n, a.shape, mybir.dt.from_np(a.dtype), kind="ExternalInput").ap() for n, a in arrays.items()}
    d["out"] = nc.dram_tensor("out", (TOKENS, E), F32, kind="ExternalOutput").ap()
    metaformer(nc, d)
    r = run_bass_kernel_spmd(nc, [{"in_" + n: a for n, a in arrays.items()}], core_ids=[0])
    return r.results[0]["out"].reshape(IMAGES, SIDE, SIDE, E)
```

```python
from contextlib import ExitStack

import numpy as np

import concourse.bass as bass
from concourse import mybir

F32 = mybir.dt.float32
F32R = mybir.dt.float32r
U32 = mybir.dt.uint32
ALU = mybir.AluOpType
ACT = mybir.ActivationFunctionType

P = 128
IMAGES, SIDE = 64, 14
POS = SIDE * SIDE
HALF = POS // 2
ROWS_HALF = SIDE // 2
TOKENS = IMAGES * POS
TILES = TOKENS // P
E = 512
EC = E // P
D = 1024
DC = D // P
HID = 2048
HC = HID // P
LL = E // 2
LC = LL // P
REL = 2 * SIDE - 1
NREL = REL * REL
W_REL = -(-NREL // 4) * 4
OT = -(-NREL // P)
CC = 16
CHUNKS = D // CC
VC = P
V_PIECES = 4
IP = IMAGES // V_PIECES
TROWS = ROWS_HALF + SIDE
GT = 4
GROUPS = -(-TILES // GT)
LN1_EPS, LN2_EPS, RMS_EPS = 1e-6, 1e-5, 1e-6


class Env:
    pass


def rel_mlp(nc, d, env):
    L = 4
    HW = W_REL // 2
    PIECE = 2048
    W1_BANKS = LC * HID // 512
    with ExitStack() as ctx:
        sb = lambda n, s, t=F32: ctx.enter_context(nc.sbuf_tensor(n, s, t))
        sem = lambda n: ctx.enter_context(nc.semaphore(n))
        pos = sb("pos", [3, W_REL])
        pos_w = sb("pos_w", [3, E])
        bias = sb("mlp_bias", [1, L - 1, E])
        gamma = sb("gamma", [P, OT])
        bout = sb("bout", [P, D])
        w = [[sb(f"mlp_w{p}{i}", [P, EC, E], F32R) for p in ("hi", "lo")] for i in range(2)]
        wout = env.wv
        H = [[sb(f"mlp_h{p}{i}", [P, EC, OT * P], F32R) for p in ("hi", "lo")] for i in range(2)]
        relu_sq = sb("mlp_relu_sq", [P, 2, 2, W_REL])
        relu, sq = relu_sq[:, 0], relu_sq[:, 1]
        T = sb("mlp_T", [P, OT * P])
        R = sb("mlp_R", [1, W_REL])
        ones = sb("ones", [P, 1])
        crms, cinv, coef = sb("mlp_crms", [P, OT]), sb("mlp_cinv", [P, OT]), sb("mlp_coef", [P, OT])
        interp = sb("interp", [P, EC, LL])
        fc1 = [relu_sq.rearrange("p a b n -> p (a b n)")[:, 0:HID], env.fc1_place]
        banks = [ctx.enter_context(nc.psum_tensor(f"mlp_ps{i}", [P, 512], F32)) for i in range(8)]
        pos_loaded, bias_loaded, small_loaded, ones_set = (sem(n) for n in ("pos_loaded", "bias_loaded", "small_loaded", "ones_set"))
        w_hi, w_lo = sem("mlp_w_hi"), sem("mlp_w_lo")
        prod, relu_ready, squared, added, lo_ready, summed, rooted = (
            sem("mlp_" + n) for n in ("prod", "relu", "squared", "added", "lo", "summed", "rooted"))
        col_summed, col_rooted, col_inverted, coef_ready = (sem("col_" + n) for n in ("summed", "rooted", "inverted", "coef"))
        gb_ready, a_prod, a_ready = sem("gb_ready"), sem("a_prod"), sem("a_ready")
        fc1_loaded, fc1_used, w1_prod = [sem(f"fc1_loaded{i}") for i in range(2)], sem("fc1_used"), sem("w1_prod")
        T_set = sem("mlp_T_set")
        w1_out = [sem("w1_out_dve"), sem("w1_out_act")]
        wv_staged, wv_hi = sem("wv_staged"), sem("wv_hi_done")

        rows = lambda name: d[name].rearrange("(k p) n -> p k n", p=P)
        pieces = [(rows(f"L0_conv_rpe_w{i + 1}"), w[i % 2][0][:], w[i % 2][1][:]) for i in range(L - 1)]
        for i in range(2):
            k = slice(i * EC // 2, (i + 1) * EC // 2)
            pieces.append((rows("L0_conv_rpe_out_w")[:, k, :], wout[0][:, k, :], wout[1][:, k, :]))
        staged = [sem(f"mlp_staged{i}") for i in range(len(pieces))]
        stage = [env.shared[:, i * PIECE:(i + 1) * PIECE].rearrange("p (k n) -> p k n", k=src.shape[1])
                 for i, (src, _, _) in enumerate(pieces)]
        SPLIT_AT = {(0, 1): 0, (1, 1): 1, (2, 0): 2, (2, 1): 3, (2, 3): 4}
        fed = interpolation().reshape(EC, P, LC, P).any(axis=(1, 3))
        last_fed = [max(k for k in range(EC) if fed[k, r]) for r in range(LC)]
        block = ctx.enter_context(nc.Block())
        half = lambda t, n: t[..., n * HW:(n + 1) * HW]

        @block.sync
        def _(sp):
            sp.dma_start(pos[:], d["rel_pos"]).then_inc(pos_loaded, 16)
            sp.dma_start(pos_w[0:2, :], d["L0_conv_rpe_pos_w"]).then_inc(pos_loaded, 16)
            sp.dma_start(pos_w[2:3, :], d["L0_conv_rpe_pos_b"].unsqueeze(0)).then_inc(pos_loaded, 16)
            for i in range(len(pieces)):
                sp.dma_start(stage[i], pieces[i][0]).then_inc(staged[i], 16)
                if i < L - 1:
                    sp.dma_start(bias[:, i, :], d[f"L0_conv_rpe_b{i + 1}"].unsqueeze(0)).then_inc(bias_loaded, 16)
            sp.dma_start(gamma[:], d["rel_gamma"]).then_inc(small_loaded, 16)
            b = d["L0_conv_rpe_out_b"]
            sp.dma_start(bout[:], bass.AP(b.tensor, 0, [[0, P], [1, D]])).then_inc(small_loaded, 16)
            sp.dma_start(interp[:], d["half_interpT"].rearrange("(k p) n -> p k n", p=P)).then_inc(small_loaded, 16)
            sp.dma_start(fc1[1], rows("fc1_wT")[:, 1, :]).then_inc(fc1_loaded[1], 16)
            sp.dma_start(env.wv_stage, rows("L0_conv_Wv")).then_inc(wv_staged, 16)
            sp.dma_start(env.ident[:], d["ident"]).then_inc(wv_staged, 16)
            for i in range(2):
                sp.dma_start(env.xA[i][:], d["x"][i * P:(i + 1) * P, :]).then_inc(env.xA_loaded[i], 16)
            sp.wait_ge(lo_ready, EC * L)
            sp.wait_ge(added, EC * L)
            sp.dma_start(fc1[0], rows("fc1_wT")[:, 0, :]).then_inc(fc1_loaded[0], 16)
            for t in range(OT):
                sp.wait_ge(a_ready, 2 * (t + 1))
                n = min(P, NREL - t * P)
                dst = bass.AP(env.a_dram.tensor, t * P * CC, [[CC, n], [NREL * CC, CHUNKS], [1, CC]])
                sp.dma_start(dst, env.a_tile[0:n, t, :].rearrange("p (k c) -> p k c", c=CC)).then_inc(env.a_stored, 16)
            for k in range(2, EC):
                sp.wait_ge(fc1_used, k - 1)
                sp.dma_start(fc1[k % 2], rows("fc1_wT")[:, k, :]).then_inc(fc1_loaded[k % 2], 16)
            for i in range(W1_BANKS):
                sp.wait_ge(w1_out[i % 2], i // 2 + 1)
                r, n = i // (HID // 512), i % (HID // 512)
                sp.dma_start(env.w1_dram[r * P:(r + 1) * P, n * 512:(n + 1) * 512], env.w1_tile[:, i, :]).then_inc(env.w1_stored, 16)

        @block.tensor
        def _(pe):
            def three(out, a, b, first, last):
                for i, (p, q) in enumerate(((0, 0), (0, 1), (1, 0))):
                    mm = nc.tensor.matmul(out, a[p], b[q], start=(first and i == 0), stop=(last and i == 2))
                return mm

            pe.wait_ge(pos_loaded, 48)
            for l in range(L):
                if l:
                    pe.wait_ge(w_lo, l)
                for m in range(EC):
                    use = EC * l + m
                    c = slice(m * P, (m + 1) * P)
                    out = [banks[2 * (use % 3) + n][:, 0:HW] for n in range(2)]
                    if use >= 3:
                        pe.wait_ge(relu_ready, 2 * (use - 2))
                        pe.wait_ge(squared, use - 2)
                    for n in range(2):
                        if l == 0:
                            nc.tensor.matmul(out[n], pos_w[:, c], half(pos, n), start=True, stop=True).then_inc(prod, 1)
                            continue
                        for k in range(EC):
                            if m == 0 and n == 0:
                                pe.wait_ge(lo_ready, EC * (l - 1) + k + 1)
                            three(out[n], [t[:, k, c] for t in w[(l - 1) % 2]], [half(t[:, k, 0:W_REL], n) for t in H[(l - 1) % 2]],
                                  k == 0, False)
                        if m == 0 and n == 0:
                            if l == 1:
                                pe.wait_ge(ones_set, 1)
                            pe.wait_ge(added, EC * l)
                            for i in range(2):
                                if l > 1:
                                    pe.wait_ge(rooted, 2 * (l - 2) + i + 1)
                                nc.tensor.matmul(banks[6 + i][0:1, 0:HW], ones[:], half(T[:, 0:W_REL], i),
                                                 start=True, stop=True).then_inc(summed, 1)
                    if l:
                        if m == 0:
                            pe.wait_ge(bias_loaded, 16 * (L - 1))
                            pe.wait_ge(rooted, 2 * l)
                        for n in range(2):
                            nc.tensor.matmul(out[n], bias[:, l - 1, c], half(R, n), start=False, stop=True).then_inc(prod, 1)
            pe.wait_ge(w_lo, len(pieces))
            for t in range(OT):
                for n in range(2):
                    if t >= 3:
                        pe.wait_ge(a_ready, 2 * (t - 3) + n + 1)
                    elif n == 0:
                        pe.wait_ge(relu_ready, 2 * EC * L)
                        pe.wait_ge(squared, EC * L)
                    for k in range(EC):
                        if t == 0 and n == 0:
                            pe.wait_ge(lo_ready, EC * (L - 1) + k + 1)
                        mm = three(banks[2 * (t % 3) + n][:], [p[:, k, t * P:(t + 1) * P] for p in H[(L - 1) % 2]],
                                   [p[:, k, n * 512:(n + 1) * 512] for p in wout], k == 0, k == EC - 1)
                    mm.then_inc(a_prod, 1)
                if t == 0:
                    pe.wait_ge(added, EC * L)
                    pe.wait_ge(rooted, 2 * (L - 1))
                    for i in range(OT):
                        mm = nc.tensor.matmul(banks[6][:, i:i + 1], T[:, i * P:(i + 1) * P], ones[:], start=True, stop=True)
                    mm.then_inc(col_summed, 1)
            pe.wait_ge(small_loaded, 48)
            pe.wait_ge(a_ready, 2 * OT)
            pe.wait_ge(col_rooted, 1)
            for k in range(EC):
                pe.wait_ge(fc1_loaded[k % 2], 16 * (k // 2 + 1))
                for r in range(LC):
                    if fed[k, r]:
                        for n in range(HID // 512):
                            mm = nc.tensor.matmul(banks[HID // 512 * r + n][:], interp[:, k, r * P:(r + 1) * P], fc1[k % 2][:, n * 512:(n + 1) * 512],
                                                  start=not fed[:k, r].any(), stop=(k == last_fed[r]))
                            if k == last_fed[r]:
                                mm.then_inc(w1_prod, 1)
                if k + 2 < EC:
                    mm.then_inc(fc1_used, 1)

        @block.scalar
        def _(act):
            for l in range(L):
                if l:
                    for n in range(2):
                        act.wait_ge(summed, 2 * (l - 1) + n + 1)
                        if l > 1 and n == 0:
                            act.wait_ge(prod, 2 * EC * l)
                        nc.scalar.activation(half(R, n), banks[6 + n][0:1, 0:HW], ACT.Sqrt, scale=1.0 / E).then_inc(rooted, 1)
                for m in range(EC):
                    use = EC * l + m
                    if use >= 2:
                        act.wait_ge(lo_ready, use - 1)
                    act.wait_ge(prod, 2 * use + 2)
                    bank = [banks[2 * (use % 3) + n][:, 0:HW] for n in range(2)]
                    for dst in (relu[:, use % 2], H[l % 2][0][:, m]):
                        for n in range(2):
                            ins = nc.scalar.activation(half(dst, n), bank[n], ACT.Relu)
                        ins.then_inc(relu_ready, 1)
                    if use >= 2:
                        act.wait_ge(added, use - 1)
                    for n in range(2):
                        ins = nc.scalar.activation(half(sq[:, use % 2], n), bank[n], ACT.Square)
                    ins.then_inc(squared, 1)
                    if (l, m) in SPLIT_AT:
                        i = SPLIT_AT[l, m]
                        act.wait_ge(staged[i], 16)
                        if i == 2:
                            act.wait_ge(prod, 2 * EC * 2)
                        nc.scalar.copy(pieces[i][1], stage[i]).then_inc(w_hi, 1)
            act.wait_ge(small_loaded, 48)
            act.wait_ge(w_lo, len(pieces))
            for t in range(OT):
                if t == 2:
                    act.wait_ge(col_summed, 1)
                    nc.scalar.activation(crms[:], banks[6][:, 0:OT], ACT.Sqrt, scale=1.0 / E).then_inc(col_rooted, 1)
                nc.scalar.activation(env.a_tile[:, t, :], bout[:], ACT.Copy, scale=gamma[:, t:t + 1]).then_inc(gb_ready, 1)
            act.wait_ge(wv_staged, 32)
            act.wait_ge(a_prod, 2 * OT)
            nc.scalar.copy(env.wv[0][:], env.wv_stage).then_inc(wv_hi, 1)
            for i in range(1, W1_BANKS, 2):
                act.wait_ge(w1_prod, i + 1)
                nc.scalar.copy(env.w1_tile[:, i, :], banks[i][:]).then_inc(w1_out[1], 1)

        @block.gpsimd
        def _(pool):
            for n, i in enumerate(SPLIT_AT.values()):
                pool.wait_ge(w_hi, n + 1)
                nc.gpsimd.tensor_tensor(pieces[i][2], stage[i], pieces[i][1].bitcast(F32), ALU.subtract).then_inc(w_lo, 1)

        @block.vector
        def _(dve):
            nc.vector.memset(ones[:], 1.0).then_inc(ones_set, 1)
            nc.vector.memset(T[:], E / P).then_inc(T_set, 1)
            for part in H[0] + H[1]:
                nc.vector.memset(part[:, :, W_REL:].bitcast(U32), 0)
            dve.wait_ge(T_set, 1)
            for l in range(L):
                for m in range(EC):
                    use = EC * l + m
                    dve.wait_ge(relu_ready, 2 * (use + 1))
                    nc.vector.tensor_tensor(H[l % 2][1][:, m, 0:W_REL], relu[:, use % 2], H[l % 2][0][:, m, 0:W_REL].bitcast(F32),
                                            ALU.subtract).then_inc(lo_ready, 1)
                    dve.wait_ge(squared, use + 1)
                    if m == 0 and l:
                        dve.wait_ge(summed, 2 * l)
                    elif m:
                        dve.wait_ge(added, use)
                    nc.vector.scalar_tensor_tensor(out=T[:, 0:W_REL], in0=T[:, 0:W_REL], scalar=RMS_EPS if m == 0 else 1.0,
                                                   in1=sq[:, use % 2], op0=ALU.mult, op1=ALU.add).then_inc(added, 1)
            dve.wait_ge(col_rooted, 1)
            nc.vector.reciprocal(cinv[:], crms[:]).then_inc(col_inverted, 1)
            dve.wait_ge(col_inverted, 1)
            dve.wait_ge(small_loaded, 48)
            nc.vector.tensor_tensor(coef[:], cinv[:], gamma[:], ALU.mult).then_inc(coef_ready, 1)
            dve.wait_ge(coef_ready, 1)
            for t in range(OT):
                dve.wait_ge(gb_ready, t + 1)
                for n in range(2):
                    dve.wait_ge(a_prod, 2 * t + n + 1)
                    a = env.a_tile[:, t, n * 512:(n + 1) * 512]
                    nc.vector.scalar_tensor_tensor(out=a, in0=banks[2 * (t % 3) + n][:], scalar=coef[:, t:t + 1],
                                                   in1=a, op0=ALU.mult, op1=ALU.add).then_inc(a_ready, 1)
            dve.wait_ge(wv_hi, 1)
            nc.vector.tensor_tensor(env.wv[1][:], env.wv_stage, env.wv[0][:].bitcast(F32), ALU.subtract)
            for i in range(0, W1_BANKS, 2):
                dve.wait_ge(w1_prod, i + 1)
                nc.vector.tensor_copy(env.w1_tile[:, i, :], banks[i][:]).then_inc(w1_out[0], 1)


def values(nc, d, env):
    with ExitStack() as ctx:
        sb = lambda n, s, t=F32: ctx.enter_context(nc.sbuf_tensor(n, s, t))
        sem = lambda n: ctx.enter_context(nc.semaphore(n))
        (wvh, wvl), ident = env.wv, env.ident
        bvb = sb("bvb", [P, D])
        minus_half = sb("minus_halfA", [P, 1])
        step_in = sb("step_inA", [P, 1])
        x, x_loaded = env.xA, env.xA_loaded
        xn = [sb(f"xnA{i}", [P, E]) for i in range(2)]
        xth = [sb(f"xthA{i}", [P, E], F32R) for i in range(2)]
        xtl = [sb(f"xtlA{i}", [P, E], F32R) for i in range(2)]
        v = [sb(f"vA{i}", [P, D]) for i in range(2)]
        stat = [sb(f"statA{i}", [P, 6]) for i in range(2)]
        mv = [sb(f"mvA{i}", [P, 2]) for i in range(2)]
        var = [sb(f"varA{i}", [P, 1]) for i in range(2)]
        rstd = [sb(f"rstdA{i}", [P, 1]) for i in range(2)]
        psT = [ctx.enter_context(nc.psum_tensor(f"psTA{i}", [P, E], F32)) for i in range(2)]
        psV = [[ctx.enter_context(nc.psum_tensor(f"psVA{i}{n}", [P, 512], F32)) for n in range(2)] for i in range(2)]
        b_loaded, const_set = sem("bv_loaded"), sem("constA")
        v_stored = [sem(f"vA_stored{i}") for i in range(2)]
        chain, mean_ready, var_ready, rstd_ready = sem("chainA"), sem("meanA"), sem("varA"), sem("rstdA")
        normed, turned, hi_ready, lo_ready = sem("normedA"), sem("turnedA"), sem("hiA"), sem("loA")
        v_prod, v_pre, v_act = sem("v_prod"), sem("v_pre"), sem("v_act")
        block = ctx.enter_context(nc.Block())
        PAIRS = TILES // 2

        def first_pair(step):
            for s in range(2):
                step(0, s, True)

        def more_pairs(eng, step, lo, hi):
            with eng.Fori(lo, hi) as j:
                for s in range(2):
                    step(j, s, False)

        @block.sync
        def _(sp):
            def load(j, s, first):
                sp.wait_ge(normed, 2 * j + s - 1)
                sp.dma_start(x[s][:], d["x"][bass.ds((2 * j + s) * P, P), :]).then_inc(x_loaded[s], 16)

            def first_v(piece):
                stored = -(-(piece + 1) * IP * POS // P)
                for s in range(2):
                    sp.wait_ge(v_stored[s], 16 * ((stored + 1 - s) // 2))
                load_v(sp, nc, env, 0, 0, piece)

            LATER = 8
            b = d["L0_conv_bv"]
            sp.dma_start(bvb[:], bass.AP(b.tensor, 0, [[0, P], [1, D]])).then_inc(b_loaded, 16)
            done = 1
            for piece in range(V_PIECES):
                upto = min((-(-(piece + 1) * IP * POS // P) + LATER) // 2, PAIRS)
                more_pairs(sp, load, done, upto)
                done = upto
                if piece == 0:
                    sp.wait_ge(env.a_stored, 16 * OT)
                    sp.wait_ge(env.w1_stored, 16 * LC * HID // 512)
                first_v(piece)
                if piece < 2:
                    load_T(sp, nc, env, piece, piece)

        @block.gpsimd
        def _(pool):
            nc.gpsimd.memset(minus_half[:], -0.5).then_inc(const_set, 1)
            pool.wait_ge(const_set, 1)

            def root(j, s, first):
                pool.wait_ge(var_ready, 2 * j + s + 1)
                if not first:
                    pool.wait_ge(normed, 2 * j + s - 1)
                nc.gpsimd.tensor_tensor(rstd[s][:], var[s][:], minus_half[:], ALU.pow).then_inc(rstd_ready, 1)

            first_pair(root)
            more_pairs(pool, root, 1, PAIRS)

        @block.vector
        def _(dve):
            def norm(j, s, first):
                t = 2 * j + s
                dve.wait_ge(x_loaded[s], 16 * (j + 1) if not first else 16)
                nc.vector.bn_stats(stat[s][:], x[s][:]).then_inc(chain, 1)
                dve.wait_ge(chain, t + 1)
                nc.vector.memset(step_in[:], 0.0)
                nc.vector.bn_aggr(mv[s][:], stat[s][:]).then_inc(mean_ready, 1)
                dve.wait_ge(mean_ready, t + 1)
                nc.vector.tensor_scalar(var[s][:], mv[s][:, 1:2], LN1_EPS, None, ALU.add).then_inc(var_ready, 1)
                dve.wait_ge(rstd_ready, t + 1)
                if not first:
                    dve.wait_ge(turned, t - 1)
                nc.vector.tensor_scalar(xn[s][:], x[s][:], mv[s][:, 0:1], rstd[s][:], ALU.subtract, ALU.mult).then_inc(normed, 1)

            def low(j, s, first):
                t = 2 * j + s
                dve.wait_ge(hi_ready, t + 1)
                if not first:
                    dve.wait_ge(v_prod, t - 1)
                nc.vector.tensor_tensor(xtl[s][:], psT[s][:], xth[s][:].bitcast(F32), ALU.subtract).then_inc(lo_ready, 1)

            def bias(j, s, first):
                t = 2 * j + s
                dve.wait_ge(v_prod, t + 1)
                if not first:
                    dve.wait_ge(v_stored[s], 16 * j)
                for n in range(2):
                    c = slice(n * 512, (n + 1) * 512)
                    nc.vector.tensor_tensor(v[s][:, c], psV[s][n][:], bvb[:, c], ALU.add).then_inc(v_pre, 1)

            norm(0, 0, True)
            norm(0, 1, True)
            low(0, 0, True)
            low(0, 1, True)
            norm(1, 0, False)
            dve.wait_ge(b_loaded, 16)
            bias(0, 0, True)
            low(1, 0, False)
            norm(1, 1, False)
            bias(0, 1, True)
            low(1, 1, False)
            with dve.Fori(1, PAIRS - 1) as j:
                for s in range(2):
                    norm(j + 1, s, False)
                    bias(j, s, False)
                    low(j + 1, s, False)
            for s in range(2):
                bias(PAIRS - 1, s, False)

        @block.tensor
        def _(pe):
            def turn(j, s, first):
                t = 2 * j + s
                pe.wait_ge(normed, t + 1)
                if not first:
                    pe.wait_ge(lo_ready, t - 1)
                for k in range(EC):
                    mm = nc.tensor.transpose(psT[s][:, k * P:(k + 1) * P], xn[s][:, k * P:(k + 1) * P], ident[:])
                mm.then_inc(turned, 1)

            def project(j, s, first):
                t = 2 * j + s
                pe.wait_ge(lo_ready, t + 1)
                if not first:
                    pe.wait_ge(v_pre, 2 * (t - 1))
                parts = [(xth[s], wvh), (xth[s], wvl), (xtl[s], wvh)]
                for n in range(2):
                    for k in range(EC):
                        for i, (a, b) in enumerate(parts):
                            mm = nc.tensor.matmul(psV[s][n][:], a[:, k * P:(k + 1) * P], b[:, k, n * 512:(n + 1) * 512],
                                                  start=(k == 0 and i == 0), stop=(k == EC - 1 and i == 2))
                mm.then_inc(v_prod, 1)

            turn(0, 0, True)
            turn(0, 1, True)
            project(0, 0, True)
            turn(1, 0, False)
            project(0, 1, True)
            turn(1, 1, False)
            with pe.Fori(1, PAIRS - 1) as j:
                for s in range(2):
                    project(j, s, False)
                    turn(j + 1, s, False)
            for s in range(2):
                project(PAIRS - 1, s, False)

        @block.scalar
        def _(act):
            def high(j, s, first):
                t = 2 * j + s
                act.wait_ge(turned, t + 1)
                if not first:
                    act.wait_ge(v_prod, t - 1)
                nc.scalar.copy(xth[s][:], psT[s][:]).then_inc(hi_ready, 1)

            def silu(j, s, first):
                t = 2 * j + s
                act.wait_ge(v_pre, 2 * (t + 1))
                nc.scalar.activation(v[s][:], v[s][:], ACT.Silu).then_inc(v_act, 1)
                act.wait_ge(v_act, t + 1)
                act.dma_start(env.v_dram[bass.ds(t * P, P), :], v[s][:]).then_inc(v_stored[s], 16)

            high(0, 0, True)
            high(0, 1, True)
            with act.Fori(1, PAIRS) as j:
                for s in range(2):
                    high(j, s, False)
                    silu(j - 1, s, False)
            for s in range(2):
                silu(PAIRS - 1, s, False)
            for s in range(2):
                act.wait_ge(v_stored[s], 16 * PAIRS)


def load_v(sp, nc, env, j, s, piece):
    for kh in range(2):
        src = env.v_dram.rearrange("(b q) c -> q b c", q=POS)[
            kh * HALF:(kh + 1) * HALF, piece * IP:(piece + 1) * IP, bass.ds((2 * j + s) * VC, VC)]
        sp.dma_start(env.v[s][:, kh, piece * IP:(piece + 1) * IP, :], src).then_inc(env.v_loaded[s], 16)


def load_T(sp, nc, env, n, par):
    for p in range(ROWS_HALF):
        src = env.a_rows[bass.ds(n, 1), p]
        sp.dma_start(env.T[par][p * SIDE:(p + 1) * SIDE].rearrange("q (r s) c -> q r (s c)", r=TROWS),
                     src.rearrange("o q r f -> (o q) r f")).then_inc(env.T_loaded[par], 16)


def token_pairs(rows, g, nt):
    return rows[bass.ds(g * GT * P, nt * P), :].rearrange("(t p e) c -> p t (e c)", p=P, e=2)


def in_pairs(t, nt):
    return t[:, 0:nt, :].rearrange("p (t e) c -> p t (e c)", e=2)


def convolve(nc, d, env):
    VCH = D // VC
    TPV = VC // CC
    HQ = CC // 2
    BANKS = HQ // 2
    with ExitStack() as ctx:
        sb = lambda n, s, t=F32: ctx.enter_context(nc.sbuf_tensor(n, s, t))
        sem = lambda n: ctx.enter_context(nc.semaphore(n))
        env.v.append(sb("vB1", [HALF, 2, IMAGES, VC]))
        v, T, v_loaded, T_loaded = env.v, env.T, env.v_loaded, env.T_loaded
        stage = env.x.rearrange("p i c -> p (i c)").rearrange("p (k n) -> p k n", n=D)
        y = [sb(f"yB{i}", [P, HQ, POS]) for i in range(2)]
        ps = [ctx.enter_context(nc.psum_tensor(f"psB{i}", [P, 512], F32)) for i in range(2 * BANKS)]
        wu_staged, wu_hi, wu_lo = sem("wu_staged"), sem("wu_hi_done"), sem("wu_lo_done")
        y_stored = [sem(f"yB_stored{i}") for i in range(2)]
        bank_ready, out_dve, out_act = sem("bank_ready"), sem("y_out_dve"), sem("y_out_act")
        block = ctx.enter_context(nc.Block())

        @block.sync
        def _(sp):
            def store_y(n, par):
                for h in range(2):
                    dst = env.y_dram.rearrange("(n h q) (b p) -> n h b q p", h=2, q=HQ, p=POS)[bass.ds(n, 1), h]
                    sp.dma_start(dst.rearrange("o b q p -> (o b) q p"), y[par][h * IMAGES:(h + 1) * IMAGES]).then_inc(y_stored[par], 16)

            def chunk(j, s, tt, first, last):
                n = 2 * TPV * j + TPV * s + tt
                if not (first and n < 2):
                    sp.wait_ge(bank_ready, BANKS * (n - 1))
                    load_T(sp, nc, env, n, tt % 2)
                if 2 <= tt < 2 + V_PIECES:
                    if s == 0:
                        load_v(sp, nc, env, j, 1, tt - 2)
                    elif not last:
                        load_v(sp, nc, env, j + 1, 0, tt - 2)
                if not (first and n < 2):
                    sp.wait_ge(out_dve, BANKS // 2 * (n - 1))
                    sp.wait_ge(out_act, BANKS // 2 * (n - 1))
                    store_y(n - 2, tt % 2)

            for i in range(2):
                if i:
                    sp.wait_ge(wu_lo, i)
                src = d["L0_conv_Wu"].rearrange("(k p) n -> p k n", p=P)[:, i * EC // 2:(i + 1) * EC // 2, :]
                sp.dma_start(stage, src).then_inc(wu_staged, 16)
            for s in range(2):
                for tt in range(TPV):
                    chunk(0, s, tt, True, False)
            sp.wait_ge(wu_lo, 2)
            sp.dma_start(in_pairs(env.x, GT), token_pairs(d["x"], 0, GT)).then_inc(env.x_loaded, 16)
            with sp.Fori(1, VCH // 2 - 1) as j:
                for s in range(2):
                    for tt in range(TPV):
                        chunk(j, s, tt, False, False)
            for s in range(2):
                for tt in range(TPV):
                    chunk(VCH // 2 - 1, s, tt, False, True)
            for n in (CHUNKS - 2, CHUNKS - 1):
                sp.wait_ge(out_dve, BANKS // 2 * (n + 1))
                sp.wait_ge(out_act, BANKS // 2 * (n + 1))
                store_y(n, n % 2)
            for s in range(2):
                sp.wait_ge(y_stored[s], 16 * CHUNKS)

        @block.tensor
        def _(pe):
            def chunk(j, s, tt, first):
                n = 2 * TPV * j + TPV * s + tt
                par = tt % 2
                if tt == 0:
                    pe.wait_ge(v_loaded[s], 2 * V_PIECES * 16 * (j + 1))
                pe.wait_ge(T_loaded[par], ROWS_HALF * 16 * (TPV * j + TPV // 2 * s + tt // 2 + 1))
                for h in range(2):
                    for qq in range(BANKS):
                        bank = ps[par * BANKS + qq]
                        if h == 0 and not (first and n < 2):
                            pe.wait_ge(out_dve if qq % 2 == 0 else out_act, BANKS // 2 * (n - 2) + qq // 2 + 1)
                        for q in (2 * qq, 2 * qq + 1):
                            for kh in range(2):
                                c = h * HQ + q
                                mm = nc.tensor.matmul(bank[h * IMAGES:(h + 1) * IMAGES, (q % 2) * POS:(q % 2 + 1) * POS],
                                                      v[s][:, kh, :, tt * CC + c],
                                                      T[par][:, kh * HALF:kh * HALF + POS, c],
                                                      start=(kh == 0), stop=(kh == 1))
                        if h == 1:
                            mm.then_inc(bank_ready, 1)

            for s in range(2):
                for tt in range(TPV):
                    chunk(0, s, tt, True)
            with pe.Fori(1, VCH // 2) as j:
                for s in range(2):
                    for tt in range(TPV):
                        chunk(j, s, tt, False)

        def evacuate(eng, copy, done, odd):
            def chunk(j, s, tt, first):
                n = 2 * TPV * j + TPV * s + tt
                par = tt % 2
                if not (first and n < 2):
                    eng.wait_ge(y_stored[par], 32 * (TPV * j + TPV // 2 * s + tt // 2))
                for qq in range(odd, BANKS, 2):
                    eng.wait_ge(bank_ready, BANKS * n + qq + 1)
                    copy(y[par][:, 2 * qq:2 * qq + 2, ::-1],
                         ps[par * BANKS + qq][:, 0:2 * POS].rearrange("p (q n) -> p q n", q=2)).then_inc(done, 1)

            for s in range(2):
                for tt in range(TPV):
                    chunk(0, s, tt, True)
            with eng.Fori(1, VCH // 2) as j:
                for s in range(2):
                    for tt in range(TPV):
                        chunk(j, s, tt, False)

        @block.vector
        def _(dve):
            for i in range(2):
                k = slice(i * EC // 2, (i + 1) * EC // 2)
                dve.wait_ge(wu_hi, i + 1)
                nc.vector.tensor_tensor(env.wu[1][:, k, :], stage, env.wu[0][:, k, :].bitcast(F32), ALU.subtract).then_inc(wu_lo, 1)
            evacuate(dve, nc.vector.tensor_copy, out_dve, 0)

        @block.scalar
        def _(act):
            for i in range(2):
                act.wait_ge(wu_staged, 16 * (i + 1))
                nc.scalar.copy(env.wu[0][:, i * EC // 2:(i + 1) * EC // 2, :], stage).then_inc(wu_hi, 1)
            evacuate(act, nc.scalar.copy, out_act, 1)


def groups(nc, d, env):
    G = GT * P
    GP = G // 2
    YR, HR = 4, 3
    with ExitStack() as ctx:
        sb = lambda n, s, t=F32: ctx.enter_context(nc.sbuf_tensor(n, s, t))
        psum = lambda n: ctx.enter_context(nc.psum_tensor(n, [P, 512], F32))
        sem = lambda n: ctx.enter_context(nc.semaphore(n))
        ident, x, x_loaded = env.ident, env.x, env.x_loaded
        bu, b1 = sb("bu", [P, DC]), sb("b1", [P, HC])
        bo, b2 = sb("bo", [P, E]), sb("b2", [P, LL])
        minus_half = sb("minus_half", [P, GT])
        step_in, half_col, warm = sb("step_in", [P, 1]), sb("half_col", [P, 1]), sb("warm", [P, 2])
        xn, x1, r = (sb(n, [P, GT, E]) for n in ("xn", "x1", "r"))
        s, s4 = sb("s", [P, GT, LL]), sb("s4", [P, GT // 2, LL])
        xth, xtl = sb("xth", [P, EC, G], F32R), sb("xtl", [P, EC, G], F32R)
        y = sb("y", [P, YR, G])
        u = sb("u", [P, 2, G])
        zh, zl = sb("zh", [P, 2, G], F32R), sb("zl", [P, 2, G], F32R)
        llh, lll = sb("llh", [P, LC, GP], F32R), sb("lll", [P, LC, GP], F32R)
        hf = sb("hf", [P, 2, GP])
        hh, hl = sb("hh", [P, HR, GP], F32R), sb("hl", [P, HR, GP], F32R)
        lln = sb("lln", [P, 2, LL])
        stat1, stat2 = sb("stat1", [P, GT, 6]), sb("stat2", [P, GT, 6])
        mv1, mv2 = sb("mv1", [P, GT, 2]), sb("mv2", [P, GT, 2])
        var1, var2, rstd1, rstd2 = (sb(n, [P, GT]) for n in ("var1", "var2", "rstd1", "rstd2"))
        acc = [psum(f"acc{i}") for i in range(GT)]
        work = [psum(f"work{i}") for i in range(2)]
        ffn = [psum(f"ffn{i}") for i in range(2)]
        const_loaded, half_set, b2_halved = sem("const_loaded"), sem("half_set"), sem("b2_halved")
        out_stored = sem("out_stored")
        y_loaded = [sem(f"y_loaded{i}") for i in range(YR)]
        stats1, means1, var1_ready, rstd1_ready = sem("stats1"), sem("means1"), sem("var1_ready"), sem("rstd1_ready")
        stats2, means2, var2_ready, rstd2_ready = sem("stats2"), sem("means2"), sem("var2_ready"), sem("rstd2_ready")
        xn_ready, turned, xth_ready, xtl_ready, bo_added = (sem(n) for n in ("xn_ready", "turned", "xth_ready", "xtl_ready", "bo_added"))
        u_prod, u_ready, z_made, zh_ready, zl_ready, wo_used, acc_ready = (
            sem(n) for n in ("u_prod", "u_ready", "z_made", "zh_ready", "zl_ready", "wo_used", "acc_ready"))
        x1_ready, xn2_ready, s_ready, r_ready = (sem(n) for n in ("x1_ready", "xn2_ready", "s_ready", "r_ready"))
        ll_prod, llh_ready, lll_ready = sem("ll_prod"), sem("llh_ready"), sem("lll_ready")
        h_prod, h_act, hl_ready, h_used = sem("h_prod"), sem("h_act"), sem("hl_ready"), sem("h_used")
        s4_ready, rest_ready, lln_ready, out_ready = sem("s4_ready"), sem("rest_ready"), sem("lln_ready"), sem("out_ready")
        warmed, col_set = sem("warmed"), sem("col_set")
        staged = [sem(f"w_staged{i}") for i in range(2)]
        w_hi, w_lo = sem("w_hi"), sem("w_lo")
        block = ctx.enter_context(nc.Block())
        x_rows = d["x"]
        out_rows = d["out"]
        CONSTS = 4

        pieces = []
        for src, (hi, lo) in ((d["L0_conv_Wo"], env.wo), (env.w1_dram, env.w1), (d["fc2_wT"], env.w2)):
            src = src.rearrange("(k p) n -> p k n", p=P)
            for i in range(2):
                k = slice(i * src.shape[1] // 2, (i + 1) * src.shape[1] // 2)
                pieces.append((src[:, k, :], hi[:, k, :], lo[:, k, :]))
        WO = 2

        def stage(i):
            k = pieces[i][0].shape[1]
            return (x1, r)[i % 2].rearrange("p i c -> p (i c)").rearrange("p (k n) -> p k n", k=k)

        def tiles(g):
            return max(0, min(GT, TILES - GT * g)) if g >= 0 else 0

        def iterations(eng, step):
            for g in range(3):
                step(g, tiles(g), tiles(g - 1), tiles(g - 2), tiles(g + 1), g)
            with eng.Fori(3, GROUPS - 2) as g:
                step(g, GT, GT, GT, GT, 3)
            for g in range(GROUPS - 2, GROUPS + 2):
                step(g, tiles(g), tiles(g - 1), tiles(g - 2), tiles(g + 1), 3)

        @block.sync
        def _(sp):
            def load_constants():
                for t, name in ((bu, "bu"), (b1, "b1")):
                    sp.dma_start(t[:], d[name]).then_inc(const_loaded, 16)
                for t, name, n in ((bo, "L0_conv_bo", E), (b2, "L0_ffn_fc2_b", LL)):
                    sp.dma_start(t[:], bass.AP(d[name].tensor, 0, [[0, P], [1, n]])).then_inc(const_loaded, 16)

            def load_x(g, nt):
                sp.dma_start(in_pairs(x, nt), token_pairs(x_rows, g, nt)).then_inc(x_loaded, 16)

            def load_y(g, m, nt):
                sp.dma_start(y[:, m % YR, 0:nt * P], env.y_dram[m * P:(m + 1) * P, bass.ds(g * G, nt * P)]).then_inc(y_loaded[m % YR], 16)

            for i, (src, _, _) in enumerate(pieces):
                if i == WO:
                    load_constants()
                    for m in range(YR):
                        load_y(0, m, GT)
                if i >= 2:
                    sp.wait_ge(w_lo, i - 1)
                sp.dma_start(stage(i), src).then_inc(staged[i % 2], 16)

            def step(g, cur, prev, last, nxt, age):
                if last:
                    sp.wait_ge(out_ready, GT // 2 * (g - 2) + last // 2)
                    sp.dma_start(token_pairs(out_rows, g - 2, last), in_pairs(r, last)).then_inc(out_stored, 16)
                if cur:
                    for m in range(YR, DC):
                        sp.wait_ge(z_made, DC * g + m - YR + 1)
                        load_y(g, m, cur)
                if nxt:
                    for m in range(YR):
                        sp.wait_ge(z_made, DC * g + m + YR + 1)
                        load_y(g + 1, m, nxt)
                    sp.wait_ge(bo_added, GT * g + cur)
                    load_x(g + 1, nxt)

            iterations(sp, step)
            sp.wait_ge(out_stored, 16 * GROUPS)

        @block.gpsimd
        def _(pool):
            nc.gpsimd.memset(minus_half[:], -0.5).then_inc(half_set, 1)
            pool.wait_ge(half_set, 1)

            def first_norm(g, nt):
                pool.wait_ge(var1_ready, g + 1)
                nc.gpsimd.tensor_tensor(rstd1[:, 0:nt], var1[:, 0:nt], minus_half[:, 0:nt], ALU.pow).then_inc(rstd1_ready, 1)

            first_norm(0, GT)
            pool.wait_ge(const_loaded, 16 * CONSTS)

            def step(g, cur, prev, last, nxt, age):
                if prev:
                    pool.wait_ge(var2_ready, g)
                    nc.gpsimd.tensor_tensor(rstd2[:, 0:prev], var2[:, 0:prev], minus_half[:, 0:prev], ALU.pow).then_inc(rstd2_ready, 1)
                for i in range(GT):
                    if i % 2 and i < prev:
                        pool.wait_ge(s_ready, GT * (g - 1) + i + 1)
                        if age >= 2:
                            pool.wait_ge(rest_ready, g - 1)
                        nc.gpsimd.tensor_tensor(s4[:, i // 2, :], s[:, i - 1, :], s[:, i, :], ALU.add).then_inc(s4_ready, 1)
                    if i < cur:
                        if i == 0:
                            pool.wait_ge(xn_ready, GT * g + cur)
                            if age == 0:
                                pool.wait_ge(w_lo, len(pieces) - 1)
                        if prev:
                            pool.wait_ge(r_ready, GT * (g - 1) + i + 1)
                        nc.gpsimd.tensor_tensor(x1[:, i, :], x[:, i, :], bo[:], ALU.add).then_inc(bo_added, 1)
                if nxt:
                    first_norm(g + 1, nxt)

            iterations(pool, step)

        @block.tensor
        def _(pe):
            def turn(g, i, age):
                pe.wait_ge(xn_ready, GT * g + i + 1)
                if age:
                    pe.wait_ge(x1_ready, GT * (g - 1) + i + 1)
                for k in range(EC):
                    mm = nc.tensor.transpose(acc[i][:, k * P:(k + 1) * P], xn[:, i, k * P:(k + 1) * P], ident[:])
                mm.then_inc(turned, 1)

            def three(out, a, b, first, last):
                for i, (p, q) in enumerate(((0, 0), (0, 1), (1, 0))):
                    mm = nc.tensor.matmul(out, a[p], b[q], start=(first and i == 0), stop=(last and i == 2))
                return mm

            def step(g, cur, prev, last, nxt, age):
                n, pairs = cur * P, prev * P // 2

                def make_u(m):
                    if m == 0:
                        pe.wait_ge(xtl_ready, GT * g + cur)
                    if m >= 2:
                        pe.wait_ge(u_ready, DC * g + m - 1)
                    elif age >= 2:
                        pe.wait_ge(h_act, 2 * HC * (g - 1))
                    for k in range(EC):
                        c = slice(m * P, (m + 1) * P)
                        mm = three(work[m % 2][:, 0:n], [w[:, k, c] for w in env.wu], [t[:, k, 0:n] for t in (xth, xtl)],
                                   k == 0, k == EC - 1)
                    mm.then_inc(u_prod, 1)

                def make_ll():
                    pe.wait_ge(s4_ready, GT // 2 * (g - 1) + prev // 2)
                    if age >= 2:
                        pe.wait_ge(lln_ready, g - 1)
                    for t in range(prev // 2):
                        for c in range(LC):
                            mm = nc.tensor.transpose(ffn[1][:, c * GP + t * P:c * GP + (t + 1) * P],
                                                     s4[:, t, c * P:(c + 1) * P], ident[:])
                    mm.then_inc(ll_prod, 1)

                def use_z(q):
                    if age == 0 and q == 0:
                        pe.wait_ge(w_lo, WO)
                    pe.wait_ge(zl_ready, DC * g + q + 1)
                    for i in range(cur):
                        t = slice(i * P, (i + 1) * P)
                        mm = three(acc[i][:], [z[:, q % 2, t] for z in (zh, zl)], [w[:, q, :] for w in env.wo], q == 0, q == DC - 1)
                        if q == DC - 1:
                            mm.then_inc(acc_ready, 1)
                        elif i == cur - 1:
                            mm.then_inc(wo_used, 1)

                def make_h(m):
                    if age == 1 and m == 0:
                        pe.wait_ge(w_lo, len(pieces))
                    if m == 0:
                        pe.wait_ge(lll_ready, g)
                    if m >= 2:
                        pe.wait_ge(h_act, 2 * (HC * (g - 1) + m - 1))
                    elif cur:
                        pe.wait_ge(u_ready, DC * g + DC - 1 + m)
                    else:
                        pe.wait_ge(h_act, 2 * HC * (g - 1))
                    for k in range(LC):
                        c = slice(m * P, (m + 1) * P)
                        mm = three(work[m % 2][:, 0:pairs], [w[:, k, c] for w in env.w1], [t[:, k, 0:pairs] for t in (llh, lll)],
                                   k == 0, k == LC - 1)
                    mm.then_inc(h_prod, 1)

                def use_h(q):
                    pe.wait_ge(hl_ready, HC * (g - 1) + q + 1)
                    for t in range(prev // 2):
                        c = slice(t * P, (t + 1) * P)
                        mm = three(ffn[t][:, 0:LL], [h[:, q % HR, c] for h in (hh, hl)], [w[:, q, :] for w in env.w2],
                                   q == 0, q == HC - 1)
                    mm.then_inc(h_used, 1)

                for m in range(DC):
                    if cur:
                        make_u(m)
                    if prev and m == DC - 1:
                        make_ll()
                    if cur and m >= 1:
                        use_z(m - 1)
                if prev:
                    make_h(0)
                    make_h(1)
                if cur:
                    use_z(DC - 1)
                for m in range(2, HC):
                    if m >= HC - GT and m - (HC - GT) < nxt:
                        turn(g + 1, m - (HC - GT), True)
                    if prev:
                        make_h(m)
                        use_h(m - 2)
                if prev:
                    use_h(HC - 2)
                    use_h(HC - 1)

            for i in range(GT):
                turn(0, i, False)
            iterations(pe, step)

        @block.scalar
        def _(act):
            def high(g, i):
                act.wait_ge(turned, GT * g + i + 1)
                nc.scalar.copy(xth[:, :, i * P:(i + 1) * P], acc[i][:].rearrange("p (k t) -> p k t", k=EC)).then_inc(xth_ready, 1)

            def split_high(i):
                act.wait_ge(staged[i % 2], 16 * (i // 2 + 1))
                nc.scalar.copy(pieces[i][1], stage(i)).then_inc(w_hi, 1)

            for i in range(WO):
                split_high(i)
            for i in range(GT):
                high(0, i)
            act.wait_ge(const_loaded, 16 * CONSTS)
            act.wait_ge(col_set, 1)

            def high_ll(g, pairs):
                act.wait_ge(ll_prod, g)
                nc.scalar.copy(llh[:, :, 0:pairs], ffn[1][:].rearrange("p (c t) -> p c t", c=LC)[:, :, 0:pairs]).then_inc(llh_ready, 1)

            def step(g, cur, prev, last, nxt, age):
                n, pairs = cur * P, prev * P // 2
                if cur:
                    for m in range(DC):
                        act.wait_ge(u_prod, DC * g + m + 1)
                        if age or m >= 2:
                            act.wait_ge(zl_ready, DC * g + m - 1)
                        nc.scalar.activation(u[:, m % 2, 0:n], work[m % 2][:, 0:n], ACT.Silu, bias=bu[:, m:m + 1]).then_inc(u_ready, 1)
                        if age == 0 and WO + m < len(pieces):
                            split_high(WO + m)
                if prev:
                    high_ll(g, pairs)
                    nc.scalar.activation(warm[:, 1:2], half_col[:], ACT.Gelu).then_inc(warmed, 1)
                for m in range(HC):
                    if m >= HC - GT and m - (HC - GT) < nxt:
                        high(g + 1, m - (HC - GT))
                    if prev:
                        act.wait_ge(h_prod, HC * (g - 1) + m + 1)
                        if age >= 2 or m >= 2:
                            act.wait_ge(hl_ready, HC * (g - 1) + m - 1)
                        if age >= 2 or m >= HR:
                            act.wait_ge(h_used, HC * (g - 1) + m - HR + 1)
                        for dst in (hf[:, m % 2, 0:pairs], hh[:, m % HR, 0:pairs]):
                            nc.scalar.activation(dst, work[m % 2][:, 0:pairs], ACT.Gelu, bias=b1[:, m:m + 1]).then_inc(h_act, 1)
                if nxt:
                    nc.scalar.activation(warm[:, 0:1], half_col[:], ACT.Silu).then_inc(warmed, 1)

            iterations(act, step)

        @block.vector
        def _(dve):

            def statistics(g, lo, hi, src, stat, done):
                for i in range(lo, hi):
                    nc.vector.bn_stats(stat[:, i, :], src[:, i, :]).then_inc(done, 1)

            def variances(g, nt, stat, stats, mv, means, var, eps, done):
                dve.wait_ge(stats, GT * g + nt)
                nc.vector.memset(step_in[:], 0.0)
                for i in range(nt):
                    nc.vector.bn_aggr(mv[:, i, :], stat[:, i, :]).then_inc(means, 1)
                dve.wait_ge(means, GT * g + nt)
                nc.vector.tensor_scalar(var[:, 0:nt], mv[:, 0:nt, 1], eps, None, ALU.add).then_inc(done, 1)

            def norm(i):
                nc.vector.tensor_scalar(xn[:, i, :], x[:, i, :], mv1[:, i, 0:1], rstd1[:, i:i + 1],
                                        ALU.subtract, ALU.mult).then_inc(xn_ready, 1)

            def low(g, i):
                dve.wait_ge(xth_ready, GT * g + i + 1)
                t = slice(i * P, (i + 1) * P)
                nc.vector.tensor_tensor(xtl[:, :, t], acc[i][:].rearrange("p (k t) -> p k t", k=EC),
                                        xth[:, :, t].bitcast(F32), ALU.subtract).then_inc(xtl_ready, 1)

            def second_norm(g, i, age):
                if age >= 2 and i == 0:
                    dve.wait_ge(s4_ready, GT // 2 * g)
                if i == 0:
                    dve.wait_ge(rstd2_ready, g + 1)
                    if age >= 2:
                        dve.wait_ge(out_stored, 16 * g)
                nc.vector.tensor_scalar(r[:, i, :], x1[:, i, :], mv2[:, i, 0:1], rstd2[:, i:i + 1],
                                        ALU.subtract, ALU.mult).then_inc(xn2_ready, 1)
                dve.wait_ge(xn2_ready, GT * g + i + 1)
                even_odd = r[:, i, :].rearrange("p (c e) -> p c e", e=2)
                nc.vector.tensor_tensor(s[:, i, :], even_odd[:, :, 0], even_odd[:, :, 1], ALU.add).then_inc(s_ready, 1)
                dve.wait_ge(s_ready, GT * g + i + 1)
                nc.vector.tensor_tensor(r[:, i, :], r[:, i, :], x1[:, i, :], ALU.add).then_inc(r_ready, 1)

            dve.wait_ge(x_loaded, 16)
            statistics(0, 0, GT, x, stat1, stats1)
            variances(0, GT, stat1, stats1, mv1, means1, var1, LN1_EPS, var1_ready)
            dve.wait_ge(rstd1_ready, 1)
            for i in range(GT):
                norm(i)

            def split_low(i):
                dve.wait_ge(w_hi, i + 1)
                nc.vector.tensor_tensor(pieces[i][2], stage(i), pieces[i][1].bitcast(F32), ALU.subtract).then_inc(w_lo, 1)

            split_low(0)
            for i in range(GT):
                low(0, i)
            for i in range(1, WO):
                split_low(i)
            nc.vector.memset(half_col[:], 0.5).then_inc(col_set, 1)
            dve.wait_ge(const_loaded, 16 * CONSTS)
            nc.vector.tensor_scalar(b2[:], b2[:], 0.5, None, ALU.mult).then_inc(b2_halved, 1)
            dve.wait_ge(b2_halved, 1)

            def next_norm(g, nt, stage):
                if stage in (0, 1):
                    if stage == 0:
                        dve.wait_ge(x_loaded, 16 * (g + 1))
                    statistics(g, 2 * stage, min(2 * stage + 2, nt), x, stat1, stats1)
                elif stage == 2:
                    variances(g, nt, stat1, stats1, mv1, means1, var1, LN1_EPS, var1_ready)
                else:
                    if stage == 3:
                        dve.wait_ge(rstd1_ready, g + 1)
                        dve.wait_ge(turned, GT * g)
                    for i in range(2 * (stage - 3), min(2 * (stage - 3) + 2, nt)):
                        norm(i)

            def first_sum(g, i):
                dve.wait_ge(acc_ready, GT * g + i + 1)
                dve.wait_ge(bo_added, GT * g + i + 1)
                nc.vector.tensor_tensor(x1[:, i, :], acc[i][:], x1[:, i, :], ALU.add).then_inc(x1_ready, 1)

            NORM_AT = (4, 5, 6, 8, 9)

            def add_sum(g, t):
                blocks = r[:, 2 * t:2 * t + 2, :].rearrange("p e (c w) -> p e c w", w=2)
                add = lln[:, t, :].unsqueeze(1).unsqueeze(3).broadcast_to([P, 2, LL, 2])
                nc.vector.tensor_tensor(blocks, blocks, add, ALU.add).then_inc(out_ready, 1)

            def step(g, cur, prev, last, nxt, age):
                n, pairs = cur * P, prev * P // 2
                for m in range(DC):
                    if m < last // 2:
                        if m == 0:
                            dve.wait_ge(lln_ready, g - 1)
                            dve.wait_ge(r_ready, GT * (g - 2) + last)
                        add_sum(g - 2, m)
                    if cur:
                        dve.wait_ge(u_ready, DC * g + m + 1)
                        dve.wait_ge(y_loaded[m % YR], 16 * (DC // YR * g + m // YR + 1))
                        z = u[:, m % 2, 0:n]
                        nc.vector.tensor_tensor(z.rearrange("c (t e p) -> c t e p", e=2, p=P), z.rearrange("c (t e p) -> c t e p", e=2, p=P),
                                                y[:, m % YR, 0:n].rearrange("c (t p e) -> c t e p", e=2, p=P), ALU.mult).then_inc(z_made, 1)
                        dve.wait_ge(z_made, DC * g + m + 1)
                        if m >= 2:
                            dve.wait_ge(wo_used, (DC - 1) * g + m - 1)
                        elif age:
                            dve.wait_ge(acc_ready, GT * g)
                        nc.vector.tensor_copy(zh[:, m % 2, 0:n], z).then_inc(zh_ready, 1)
                        dve.wait_ge(zh_ready, DC * g + m + 1)
                        nc.vector.tensor_tensor(zl[:, m % 2, 0:n], z, zh[:, m % 2, 0:n].bitcast(F32), ALU.subtract).then_inc(zl_ready, 1)
                        if age == 0 and WO + m < len(pieces):
                            split_low(WO + m)
                    if prev:
                        if 0 < m < 3:
                            dve.wait_ge(x1_ready, GT * (g - 1) + prev)
                            statistics(g - 1, 2 * m - 2, min(2 * m, prev), x1, stat2, stats2)
                            if m == 2:
                                variances(g - 1, prev, stat2, stats2, mv2, means2, var2, LN2_EPS, var2_ready)
                        elif 3 <= m < 3 + prev:
                            second_norm(g - 1, m - 3, age)
                        if m == DC - 1:
                            dve.wait_ge(llh_ready, g)
                            nc.vector.tensor_tensor(lll[:, :, 0:pairs], ffn[1][:].rearrange("p (c t) -> p c t", c=LC)[:, :, 0:pairs],
                                                    llh[:, :, 0:pairs].bitcast(F32), ALU.subtract).then_inc(lll_ready, 1)
                            if last:
                                dve.wait_ge(out_ready, GT // 2 * (g - 1))
                            for t in range(prev // 2):
                                ins = nc.vector.scalar_tensor_tensor(out=lln[:, t, :], in0=s4[:, t, :], scalar=-0.25, in1=b2[:],
                                                                     op0=ALU.mult, op1=ALU.add)
                            ins.then_inc(rest_ready, 1)
                for m in range(HC):
                    if prev:
                        dve.wait_ge(h_act, 2 * (HC * (g - 1) + m + 1))
                        if age >= 2 or m >= HR:
                            dve.wait_ge(h_used, HC * (g - 1) + m - HR + 1)
                        nc.vector.tensor_tensor(hl[:, m % HR, 0:pairs], hf[:, m % 2, 0:pairs], hh[:, m % HR, 0:pairs].bitcast(F32),
                                                ALU.subtract).then_inc(hl_ready, 1)
                    if m < cur:
                        first_sum(g, m)
                    if nxt and m in NORM_AT:
                        next_norm(g + 1, nxt, NORM_AT.index(m))
                    if m >= HC - GT and m - (HC - GT) < nxt:
                        low(g + 1, m - (HC - GT))
                if prev:
                    dve.wait_ge(h_used, HC * g)
                    dve.wait_ge(rest_ready, g)
                    for t in range(prev // 2):
                        ins = nc.vector.scalar_tensor_tensor(out=lln[:, t, :], in0=ffn[t][:, 0:LL], scalar=0.5, in1=lln[:, t, :],
                                                             op0=ALU.mult, op1=ALU.add)
                    ins.then_inc(lln_ready, 1)

            iterations(dve, step)


def metaformer(nc, d):
    env = Env()
    env.a_dram = nc.dram_tensor("rel_kernel", [CHUNKS, NREL, CC], F32).ap()
    env.v_dram = nc.dram_tensor("v_scratch", [TOKENS, D], F32).ap()
    env.y_dram = nc.dram_tensor("y_scratch", [D, TOKENS], F32).ap()
    env.a_rows = bass.AP(env.a_dram.tensor, 0, [[NREL * CC, CHUNKS], [REL * CC, ROWS_HALF], [CC, SIDE], [REL * CC, TROWS], [1, SIDE * CC]])
    env.w1_dram = nc.dram_tensor("w1_scratch", [LL, HID], F32).ap()
    with ExitStack() as ctx:
        sem = lambda n: ctx.enter_context(nc.semaphore(n))
        env.a_stored, env.w1_stored = sem("a_stored"), sem("w1_stored")
        env.v_loaded, env.T_loaded = ([sem(f"{n}_loaded{i}") for i in range(2)] for n in ("v", "T"))
        env.x_loaded = sem("x_loaded")
        env.xA_loaded = [sem(f"xA_loaded{i}") for i in range(2)]
        parts = lambda n, s, **side: [ctx.enter_context(nc.sbuf_tensor(f"{n}_{part}", s, F32R, **side)) for part in ("hi", "lo")]
        env.ident = ctx.enter_context(nc.sbuf_tensor("ident", [P, P], F32, side="right"))
        with ExitStack() as first:
            sb = lambda n, s, t=F32: first.enter_context(nc.sbuf_tensor(n, s, t))
            shared = env.shared = sb("v_chunk0", [P, 2 * IMAGES * VC])
            place = lambda at, n: shared[:, at:at + n]
            env.a_tile = place(0, OT * D).rearrange("p (t n) -> p t n", n=D)
            env.w1_tile = place(OT * D, LC * HID).rearrange("p (i n) -> p i n", n=512)
            env.wv_stage = place(OT * D + LC * HID, EC * D).rearrange("p (k n) -> p k n", n=D)
            env.fc1_place = place(OT * D + LC * HID + EC * D, HID)
            env.v = [shared[0:HALF, :].rearrange("p (h b c) -> p h b c", h=2, c=VC)]
            with ExitStack() as second:
                env.wv = [second.enter_context(nc.sbuf_tensor(n, [P, EC, D], F32R, side="right")) for n in ("wv_hi", "wv_lo")]
                env.xA = [second.enter_context(nc.sbuf_tensor(f"xA{i}", [P, E], F32, side="right")) for i in range(2)]
                rel_mlp(nc, d, env)
                env.T = [sb(f"T{i}", [HALF, TROWS * SIDE, CC]) for i in range(2)]
                values(nc, d, env)
            env.x = ctx.enter_context(nc.sbuf_tensor("x", [P, GT, E], F32, side="right"))
            env.wu = parts("wu", [P, EC, D], side="right")
            convolve(nc, d, env)
        env.wo = parts("wo", [P, DC, E])
        env.w1, env.w2 = parts("w1", [P, LC, HID]), parts("w2", [P, HC, LL])
        groups(nc, d, env)


def interpolation():
    at = np.linspace(0.0, 1.0, E, dtype=np.float32) * np.float32(LL - 1)
    i0 = np.clip(np.floor(at).astype(np.int32), 0, LL - 2)
    w = at - i0.astype(np.float32)
    interp = np.zeros((E, LL), np.float32)
    interp[np.arange(E), i0] = np.float32(1.0) - w
    interp[np.arange(E), i0 + 1] = w
    return interp


def constants():
    c = {"ident": np.eye(P, dtype=np.float32)}
    c["half_interpT"] = interpolation() * np.float32(0.5)
    away = (SIDE - 1 - np.arange(REL)).astype(np.float32)
    di, dj = np.meshgrid(away, away, indexing="ij")
    c["rel_pos"] = np.pad(np.stack([di.ravel(), dj.ravel(), np.ones(NREL, np.float32)]), ((0, 0), (0, W_REL - NREL)))
    g = np.float32(0.999) ** (np.abs(di) + np.abs(dj)).ravel()
    gamma = np.zeros(OT * P, np.float32)
    gamma[:NREL] = g
    c["rel_gamma"] = np.ascontiguousarray(gamma.reshape(OT, P).T)
    return c


def kernel(**inputs):
    import concourse.bacc as bacc
    from concourse.bass_utils import run_bass_kernel_spmd

    arrays = {name: np.ascontiguousarray(a) for name, a in inputs.items()}
    arrays["x"] = arrays["x"].reshape(TOKENS, E)
    cols = lambda a, n: np.ascontiguousarray(np.asarray(a).reshape(n, P).T)
    arrays["bu"] = cols(arrays.pop("L0_conv_bu"), DC)
    arrays["b1"] = cols(arrays.pop("L0_ffn_fc1_b"), HC)
    arrays["fc1_wT"] = np.ascontiguousarray(arrays.pop("L0_ffn_fc1_w").T)
    arrays["fc2_wT"] = np.ascontiguousarray(arrays.pop("L0_ffn_fc2_w").T)
    arrays.update(constants())
    nc = bacc.Bacc("TRN2", target_bir_lowering=False, num_devices=1, dynamic_dma_scratch_size=1024)
    d = {n: nc.dram_tensor("in_" + n, a.shape, mybir.dt.from_np(a.dtype), kind="ExternalInput").ap() for n, a in arrays.items()}
    d["out"] = nc.dram_tensor("out", (TOKENS, E), F32, kind="ExternalOutput").ap()
    metaformer(nc, d)
    r = run_bass_kernel_spmd(nc, [{"in_" + n: a for n, a in arrays.items()}], core_ids=[0])
    return r.results[0]["out"].reshape(IMAGES, SIDE, SIDE, E)
```

```python
from contextlib import ExitStack

import numpy as np

import concourse.bass as bass
from concourse import mybir

F32 = mybir.dt.float32
F32R = mybir.dt.float32r
U32 = mybir.dt.uint32
ALU = mybir.AluOpType
ACT = mybir.ActivationFunctionType

P = 128
IMAGES, SIDE = 64, 14
POS = SIDE * SIDE
HALF = POS // 2
ROWS_HALF = SIDE // 2
TOKENS = IMAGES * POS
TILES = TOKENS // P
E = 512
EC = E // P
D = 1024
DC = D // P
HID = 2048
HC = HID // P
LL = E // 2
LC = LL // P
REL = 2 * SIDE - 1
NREL = REL * REL
W_REL = -(-NREL // 4) * 4
OT = -(-NREL // P)
CC = 16
CHUNKS = D // CC
VC = P
V_PIECES = 4
FIRST_PIECES = (0, 20, 40, 58, IMAGES)
MORE_PIECES = tuple(range(0, IMAGES + 1, IMAGES // V_PIECES))
TROWS = ROWS_HALF + SIDE
GT = 4
GROUPS = -(-TILES // GT)
LN1_EPS, LN2_EPS, RMS_EPS = 1e-6, 1e-5, 1e-6


class Env:
    pass


def pair_rows(rows, j, s):
    return rows[bass.ds(j * 2 * P, 2 * P), :].rearrange("(p e) c -> p e c", e=2)[:, s, :]


def rel_mlp(nc, d, env):
    L = 4
    HW = W_REL // 2
    PIECE = 2048
    W1_BANKS = LC * HID // 512
    with ExitStack() as ctx:
        sb = lambda n, s, t=F32: ctx.enter_context(nc.sbuf_tensor(n, s, t))
        sem = lambda n: ctx.enter_context(nc.semaphore(n))
        pos = sb("pos", [3, W_REL])
        pos_w = sb("pos_w", [3, E])
        bias = sb("mlp_bias", [1, L - 1, E])
        gamma = sb("gamma", [P, OT])
        bout = sb("bout", [P, D])
        w = [[sb(f"mlp_w{p}{i}", [P, EC, E], F32R) for p in ("hi", "lo")] for i in range(2)]
        wout = env.wv
        H = [[sb(f"mlp_h{p}{i}", [P, EC, OT * P], F32R) for p in ("hi", "lo")] for i in range(2)]
        relu_sq = sb("mlp_relu_sq", [P, 2, 2, W_REL])
        relu, sq = relu_sq[:, 0], relu_sq[:, 1]
        T = sb("mlp_T", [P, OT * P])
        R = sb("mlp_R", [1, W_REL])
        ones = sb("ones", [P, 1])
        crms, cinv, coef = sb("mlp_crms", [P, OT]), sb("mlp_cinv", [P, OT]), sb("mlp_coef", [P, OT])
        interp = sb("interp", [P, EC, LL])
        fc1 = [relu_sq.rearrange("p a b n -> p (a b n)")[:, 0:HID], env.fc1_place]
        banks = [ctx.enter_context(nc.psum_tensor(f"mlp_ps{i}", [P, 512], F32)) for i in range(8)]
        pos_loaded, bias_loaded, small_loaded, ones_set = (sem(n) for n in ("pos_loaded", "bias_loaded", "small_loaded", "ones_set"))
        w_hi, w_lo = sem("mlp_w_hi"), sem("mlp_w_lo")
        prod, relu_ready, squared, added, lo_ready, summed, rooted = (
            sem("mlp_" + n) for n in ("prod", "relu", "squared", "added", "lo", "summed", "rooted"))
        col_summed, col_rooted, col_inverted, coef_ready = (sem("col_" + n) for n in ("summed", "rooted", "inverted", "coef"))
        gb_ready, a_prod, a_ready = sem("gb_ready"), sem("a_prod"), sem("a_ready")
        fc1_loaded, fc1_used, w1_prod = [sem(f"fc1_loaded{i}") for i in range(2)], sem("fc1_used"), sem("w1_prod")
        T_set = sem("mlp_T_set")
        w1_out = [sem("w1_out_dve"), sem("w1_out_act")]
        wv_staged, wv_hi = sem("wv_staged"), sem("wv_hi_done")

        rows = lambda name: d[name].rearrange("(k p) n -> p k n", p=P)
        pieces = [(rows(f"L0_conv_rpe_w{i + 1}"), w[i % 2][0][:], w[i % 2][1][:]) for i in range(L - 1)]
        for i in range(2):
            k = slice(i * EC // 2, (i + 1) * EC // 2)
            pieces.append((rows("L0_conv_rpe_out_w")[:, k, :], wout[0][:, k, :], wout[1][:, k, :]))
        staged = [sem(f"mlp_staged{i}") for i in range(len(pieces))]
        stage = [env.shared[:, i * PIECE:(i + 1) * PIECE].rearrange("p (k n) -> p k n", k=src.shape[1])
                 for i, (src, _, _) in enumerate(pieces)]
        SPLIT_AT = {(0, 1): 0, (1, 1): 1, (2, 0): 2, (2, 1): 3, (2, 3): 4}
        fed = interpolation().reshape(EC, P, LC, P).any(axis=(1, 3))
        last_fed = [max(k for k in range(EC) if fed[k, r]) for r in range(LC)]
        block = ctx.enter_context(nc.Block())
        half = lambda t, n: t[..., n * HW:(n + 1) * HW]

        @block.sync
        def _(sp):
            sp.dma_start(pos[:], d["rel_pos"]).then_inc(pos_loaded, 16)
            sp.dma_start(pos_w[0:2, :], d["L0_conv_rpe_pos_w"]).then_inc(pos_loaded, 16)
            sp.dma_start(pos_w[2:3, :], d["L0_conv_rpe_pos_b"].unsqueeze(0)).then_inc(pos_loaded, 16)
            for i in range(len(pieces)):
                sp.dma_start(stage[i], pieces[i][0]).then_inc(staged[i], 16)
                if i < L - 1:
                    sp.dma_start(bias[:, i, :], d[f"L0_conv_rpe_b{i + 1}"].unsqueeze(0)).then_inc(bias_loaded, 16)
            sp.dma_start(gamma[:], d["rel_gamma"]).then_inc(small_loaded, 16)
            b = d["L0_conv_rpe_out_b"]
            sp.dma_start(bout[:], bass.AP(b.tensor, 0, [[0, P], [1, D]])).then_inc(small_loaded, 16)
            sp.dma_start(interp[:], d["half_interpT"].rearrange("(k p) n -> p k n", p=P)).then_inc(small_loaded, 16)
            sp.dma_start(fc1[1], rows("fc1_wT")[:, 1, :]).then_inc(fc1_loaded[1], 16)
            sp.dma_start(env.wv_stage, rows("L0_conv_Wv")).then_inc(wv_staged, 16)
            sp.dma_start(env.ident[:], d["ident"]).then_inc(wv_staged, 16)
            for i in range(2):
                sp.dma_start(env.xA[i][:], pair_rows(d["x"], 0, i)).then_inc(env.xA_loaded[i], 16)
            sp.wait_ge(lo_ready, EC * L)
            sp.wait_ge(added, EC * L)
            sp.dma_start(fc1[0], rows("fc1_wT")[:, 0, :]).then_inc(fc1_loaded[0], 16)
            for t in range(OT):
                sp.wait_ge(a_ready, 2 * (t + 1))
                n = min(P, NREL - t * P)
                dst = bass.AP(env.a_dram.tensor, t * P * CC, [[CC, n], [NREL * CC, CHUNKS], [1, CC]])
                sp.dma_start(dst, env.a_tile[0:n, t, :].rearrange("p (k c) -> p k c", c=CC)).then_inc(env.a_stored, 16)
            for k in range(2, EC):
                sp.wait_ge(fc1_used, k - 1)
                sp.dma_start(fc1[k % 2], rows("fc1_wT")[:, k, :]).then_inc(fc1_loaded[k % 2], 16)
            for i in range(W1_BANKS):
                sp.wait_ge(w1_out[i % 2], i // 2 + 1)
                r, n = i // (HID // 512), i % (HID // 512)
                sp.dma_start(env.w1_dram[r * P:(r + 1) * P, n * 512:(n + 1) * 512], env.w1_tile[:, i, :]).then_inc(env.w1_stored, 16)

        @block.tensor
        def _(pe):
            def three(out, a, b, first, last):
                for i, (p, q) in enumerate(((0, 0), (0, 1), (1, 0))):
                    mm = nc.tensor.matmul(out, a[p], b[q], start=(first and i == 0), stop=(last and i == 2))
                return mm

            pe.wait_ge(pos_loaded, 48)
            for l in range(L):
                if l:
                    pe.wait_ge(w_lo, l)
                for m in range(EC):
                    use = EC * l + m
                    c = slice(m * P, (m + 1) * P)
                    out = [banks[2 * (use % 3) + n][:, 0:HW] for n in range(2)]
                    if use >= 3:
                        pe.wait_ge(relu_ready, 2 * (use - 2))
                        pe.wait_ge(squared, use - 2)
                    for n in range(2):
                        if l == 0:
                            nc.tensor.matmul(out[n], pos_w[:, c], half(pos, n), start=True, stop=True).then_inc(prod, 1)
                            continue
                        for k in range(EC):
                            if m == 0 and n == 0:
                                pe.wait_ge(lo_ready, EC * (l - 1) + k + 1)
                            three(out[n], [t[:, k, c] for t in w[(l - 1) % 2]], [half(t[:, k, 0:W_REL], n) for t in H[(l - 1) % 2]],
                                  k == 0, False)
                        if m == 0 and n == 0:
                            if l == 1:
                                pe.wait_ge(ones_set, 1)
                            pe.wait_ge(added, EC * l)
                            for i in range(2):
                                if l > 1:
                                    pe.wait_ge(rooted, 2 * (l - 2) + i + 1)
                                nc.tensor.matmul(banks[6 + i][0:1, 0:HW], ones[:], half(T[:, 0:W_REL], i),
                                                 start=True, stop=True).then_inc(summed, 1)
                    if l:
                        if m == 0:
                            pe.wait_ge(bias_loaded, 16 * (L - 1))
                            pe.wait_ge(rooted, 2 * l)
                        for n in range(2):
                            nc.tensor.matmul(out[n], bias[:, l - 1, c], half(R, n), start=False, stop=True).then_inc(prod, 1)
            pe.wait_ge(w_lo, len(pieces))
            for t in range(OT):
                for n in range(2):
                    if t >= 3:
                        pe.wait_ge(a_ready, 2 * (t - 3) + n + 1)
                    elif n == 0:
                        pe.wait_ge(relu_ready, 2 * EC * L)
                        pe.wait_ge(squared, EC * L)
                    for k in range(EC):
                        if t == 0 and n == 0:
                            pe.wait_ge(lo_ready, EC * (L - 1) + k + 1)
                        mm = three(banks[2 * (t % 3) + n][:], [p[:, k, t * P:(t + 1) * P] for p in H[(L - 1) % 2]],
                                   [p[:, k, n * 512:(n + 1) * 512] for p in wout], k == 0, k == EC - 1)
                    mm.then_inc(a_prod, 1)
                if t == 0:
                    pe.wait_ge(added, EC * L)
                    pe.wait_ge(rooted, 2 * (L - 1))
                    for i in range(OT):
                        mm = nc.tensor.matmul(banks[6][:, i:i + 1], T[:, i * P:(i + 1) * P], ones[:], start=True, stop=True)
                    mm.then_inc(col_summed, 1)
            pe.wait_ge(small_loaded, 48)
            pe.wait_ge(a_ready, 2 * OT)
            pe.wait_ge(col_rooted, 1)
            for k in range(EC):
                pe.wait_ge(fc1_loaded[k % 2], 16 * (k // 2 + 1))
                for r in range(LC):
                    if fed[k, r]:
                        for n in range(HID // 512):
                            mm = nc.tensor.matmul(banks[HID // 512 * r + n][:], interp[:, k, r * P:(r + 1) * P], fc1[k % 2][:, n * 512:(n + 1) * 512],
                                                  start=not fed[:k, r].any(), stop=(k == last_fed[r]))
                            if k == last_fed[r]:
                                mm.then_inc(w1_prod, 1)
                if k + 2 < EC:
                    mm.then_inc(fc1_used, 1)

        @block.scalar
        def _(act):
            for l in range(L):
                if l:
                    for n in range(2):
                        act.wait_ge(summed, 2 * (l - 1) + n + 1)
                        if l > 1 and n == 0:
                            act.wait_ge(prod, 2 * EC * l)
                        nc.scalar.activation(half(R, n), banks[6 + n][0:1, 0:HW], ACT.Sqrt, scale=1.0 / E).then_inc(rooted, 1)
                for m in range(EC):
                    use = EC * l + m
                    if use >= 2:
                        act.wait_ge(lo_ready, use - 1)
                    act.wait_ge(prod, 2 * use + 2)
                    bank = [banks[2 * (use % 3) + n][:, 0:HW] for n in range(2)]
                    for dst in (relu[:, use % 2], H[l % 2][0][:, m]):
                        for n in range(2):
                            ins = nc.scalar.activation(half(dst, n), bank[n], ACT.Relu)
                        ins.then_inc(relu_ready, 1)
                    if use >= 2:
                        act.wait_ge(added, use - 1)
                    for n in range(2):
                        ins = nc.scalar.activation(half(sq[:, use % 2], n), bank[n], ACT.Square)
                    ins.then_inc(squared, 1)
                    if (l, m) in SPLIT_AT:
                        i = SPLIT_AT[l, m]
                        act.wait_ge(staged[i], 16)
                        if i == 2:
                            act.wait_ge(prod, 2 * EC * 2)
                        nc.scalar.copy(pieces[i][1], stage[i]).then_inc(w_hi, 1)
            act.wait_ge(small_loaded, 48)
            act.wait_ge(w_lo, len(pieces))
            for t in range(OT):
                if t == 2:
                    act.wait_ge(col_summed, 1)
                    nc.scalar.activation(crms[:], banks[6][:, 0:OT], ACT.Sqrt, scale=1.0 / E).then_inc(col_rooted, 1)
                nc.scalar.activation(env.a_tile[:, t, :], bout[:], ACT.Copy, scale=gamma[:, t:t + 1]).then_inc(gb_ready, 1)
            act.wait_ge(wv_staged, 32)
            act.wait_ge(a_prod, 2 * OT)
            nc.scalar.copy(env.wv[0][:], env.wv_stage).then_inc(wv_hi, 1)
            for i in range(1, W1_BANKS, 2):
                act.wait_ge(w1_prod, i + 1)
                nc.scalar.copy(env.w1_tile[:, i, :], banks[i][:]).then_inc(w1_out[1], 1)

        @block.gpsimd
        def _(pool):
            for n, i in enumerate(SPLIT_AT.values()):
                pool.wait_ge(w_hi, n + 1)
                nc.gpsimd.tensor_tensor(pieces[i][2], stage[i], pieces[i][1].bitcast(F32), ALU.subtract).then_inc(w_lo, 1)

        @block.vector
        def _(dve):
            nc.vector.memset(ones[:], 1.0).then_inc(ones_set, 1)
            nc.vector.memset(T[:], E / P).then_inc(T_set, 1)
            for part in H[0] + H[1]:
                nc.vector.memset(part[:, :, W_REL:].bitcast(U32), 0)
            dve.wait_ge(T_set, 1)
            for l in range(L):
                for m in range(EC):
                    use = EC * l + m
                    dve.wait_ge(relu_ready, 2 * (use + 1))
                    nc.vector.tensor_tensor(H[l % 2][1][:, m, 0:W_REL], relu[:, use % 2], H[l % 2][0][:, m, 0:W_REL].bitcast(F32),
                                            ALU.subtract).then_inc(lo_ready, 1)
                    dve.wait_ge(squared, use + 1)
                    if m == 0 and l:
                        dve.wait_ge(summed, 2 * l)
                    elif m:
                        dve.wait_ge(added, use)
                    nc.vector.scalar_tensor_tensor(out=T[:, 0:W_REL], in0=T[:, 0:W_REL], scalar=RMS_EPS if m == 0 else 1.0,
                                                   in1=sq[:, use % 2], op0=ALU.mult, op1=ALU.add).then_inc(added, 1)
            dve.wait_ge(col_rooted, 1)
            nc.vector.reciprocal(cinv[:], crms[:]).then_inc(col_inverted, 1)
            dve.wait_ge(col_inverted, 1)
            dve.wait_ge(small_loaded, 48)
            nc.vector.tensor_tensor(coef[:], cinv[:], gamma[:], ALU.mult).then_inc(coef_ready, 1)
            dve.wait_ge(coef_ready, 1)
            for t in range(OT):
                dve.wait_ge(gb_ready, t + 1)
                for n in range(2):
                    dve.wait_ge(a_prod, 2 * t + n + 1)
                    a = env.a_tile[:, t, n * 512:(n + 1) * 512]
                    nc.vector.scalar_tensor_tensor(out=a, in0=banks[2 * (t % 3) + n][:], scalar=coef[:, t:t + 1],
                                                   in1=a, op0=ALU.mult, op1=ALU.add).then_inc(a_ready, 1)
            dve.wait_ge(wv_hi, 1)
            nc.vector.tensor_tensor(env.wv[1][:], env.wv_stage, env.wv[0][:].bitcast(F32), ALU.subtract)
            for i in range(0, W1_BANKS, 2):
                dve.wait_ge(w1_prod, i + 1)
                nc.vector.tensor_copy(env.w1_tile[:, i, :], banks[i][:]).then_inc(w1_out[0], 1)


def values(nc, d, env):
    with ExitStack() as ctx:
        sb = lambda n, s, t=F32: ctx.enter_context(nc.sbuf_tensor(n, s, t))
        sem = lambda n: ctx.enter_context(nc.semaphore(n))
        (wvh, wvl), ident = env.wv, env.ident
        bvb = sb("bvb", [P, D])
        minus_half = sb("minus_halfA", [P, 1])
        step_in, warm = sb("step_inA", [P, 1]), sb("warmA", [P, 1])
        x, x_loaded = env.xA, env.xA_loaded
        xn = [sb(f"xnA{i}", [P, E]) for i in range(2)]
        xth = [sb(f"xthA{i}", [P, E], F32R) for i in range(2)]
        xtl = [sb(f"xtlA{i}", [P, E], F32R) for i in range(2)]
        xt = [sb(f"xtA{i}", [P, E]) for i in range(2)]
        v = [sb(f"vA{i}", [P, D]) for i in range(2)]
        stat = [sb(f"statA{i}", [P, 6]) for i in range(2)]
        mv = [sb(f"mvA{i}", [P, 2]) for i in range(2)]
        var = [sb(f"varA{i}", [P, 1]) for i in range(2)]
        rstd = [sb(f"rstdA{i}", [P, 1]) for i in range(2)]
        psT = [ctx.enter_context(nc.psum_tensor(f"psTA{i}", [P, E], F32)) for i in range(2)]
        psV = [[ctx.enter_context(nc.psum_tensor(f"psVA{i}{n}", [P, 512], F32)) for n in range(2)] for i in range(2)]
        b_loaded, const_set = sem("bv_loaded"), sem("constA")
        WU_AFTER = 4
        WU_PARTS = EC
        wu_stage = env.xt.rearrange("p i c -> p (i c)").rearrange("p (k n) -> p k n", n=D)
        wu_staged, wu_hi, wu_lo = sem("wu_staged"), sem("wu_hi_done"), sem("wu_lo_done")
        v_stored = [sem(f"vA_stored{i}") for i in range(2)]
        chain, mean_ready, var_ready, rstd_ready = sem("chainA"), sem("meanA"), sem("varA"), sem("rstdA")
        normed, turned, hi_ready, lo_ready = sem("normedA"), sem("turnedA"), sem("hiA"), sem("loA")
        v_prod, v_pre, v_act = sem("v_prod"), sem("v_pre"), sem("v_act")
        xt_ready, xt_stored = sem("xtA_ready"), [sem(f"xtA_stored{i}") for i in range(2)]
        block = ctx.enter_context(nc.Block())
        PAIRS = TILES // 2

        def pairs_of(piece):
            return -(-FIRST_PIECES[piece + 1] * POS // (2 * P))

        def before_pair(piece):
            return min(pairs_of(piece) + 3, PAIRS)

        def first_pair(step):
            for s in range(2):
                step(0, s, True)

        def more_pairs(eng, step, lo, hi):
            with eng.Fori(lo, hi) as j:
                for s in range(2):
                    step(j, s, False)

        @block.sync
        def _(sp):
            def load(j, s, first):
                sp.wait_ge(normed, 2 * j + s - 1)
                sp.dma_start(x[s][:], pair_rows(d["x"], j, s)).then_inc(x_loaded[s], 16)

            def first_v(piece):
                for s in range(2):
                    sp.wait_ge(v_stored[s], 16 * pairs_of(piece))
                load_v(sp, nc, env, 0, 0, piece, FIRST_PIECES)

            b = d["L0_conv_bv"]
            sp.dma_start(bvb[:], bass.AP(b.tensor, 0, [[0, P], [1, D]])).then_inc(b_loaded, 16)

            def first_wu(half):
                if half:
                    sp.wait_ge(wu_lo, WU_PARTS // 2)
                src = d["L0_conv_Wu"].rearrange("(k p) n -> p k n", p=P)[:, half * EC // 2:(half + 1) * EC // 2, :]
                sp.dma_start(wu_stage, src).then_inc(wu_staged, 16)

            def first_xt():
                sp.wait_ge(wu_lo, WU_PARTS)
                for s in range(2):
                    sp.wait_ge(xt_stored[s], 16 * (GT // 2))
                load_xt(sp, env, 0, GT)

            sp.wait_ge(env.a_stored, 16 * OT)
            sp.wait_ge(env.w1_stored, 16 * LC * HID // 512)
            done = 1
            for i in range(2):
                at = before_pair(i)
                more_pairs(sp, load, done, at)
                first_v(i)
                more_pairs(sp, load, at, at + 2)
                load_T(sp, nc, env, i, i)
                more_pairs(sp, load, at + 2, at + WU_AFTER)
                first_wu(i)
                done = at + WU_AFTER
            more_pairs(sp, load, done, done + 6)
            first_xt()
            more_pairs(sp, load, done + 6, before_pair(2))
            first_v(2)
            more_pairs(sp, load, before_pair(2), PAIRS)
            first_v(3)

        @block.gpsimd
        def _(pool):
            nc.gpsimd.memset(minus_half[:], -0.5).then_inc(const_set, 1)
            pool.wait_ge(const_set, 1)

            def root(j, s, first):
                pool.wait_ge(var_ready, 2 * j + s + 1)
                if not first:
                    pool.wait_ge(normed, 2 * j + s - 1)
                nc.gpsimd.tensor_tensor(rstd[s][:], var[s][:], minus_half[:], ALU.pow).then_inc(rstd_ready, 1)

            first_pair(root)
            done = 1
            for i in range(WU_PARTS):
                upto = before_pair(2 * i // WU_PARTS) + WU_AFTER + 1 + 2 * (i % (WU_PARTS // 2))
                more_pairs(pool, root, done, upto)
                done = upto
                pool.wait_ge(wu_staged, 16 * (2 * i // WU_PARTS + 1))
                k = slice(i * EC // WU_PARTS, (i + 1) * EC // WU_PARTS)
                staged = wu_stage[:, i % (WU_PARTS // 2), :].unsqueeze(1)
                nc.gpsimd.tensor_copy(env.wu[0][:, k, :], staged).then_inc(wu_hi, 1)
                root(upto, 0, False)
                pool.wait_ge(wu_hi, i + 1)
                nc.gpsimd.tensor_tensor(env.wu[1][:, k, :], staged, env.wu[0][:, k, :].bitcast(F32), ALU.subtract).then_inc(wu_lo, 1)
                root(upto, 1, False)
                done = upto + 1
            more_pairs(pool, root, done, PAIRS)

        @block.vector
        def _(dve):
            def norm(j, s, first):
                t = 2 * j + s
                dve.wait_ge(x_loaded[s], 16 * (j + 1) if not first else 16)
                nc.vector.bn_stats(stat[s][:], x[s][:]).then_inc(chain, 1)
                dve.wait_ge(chain, t + 1)
                nc.vector.memset(step_in[:], 0.0)
                nc.vector.bn_aggr(mv[s][:], stat[s][:]).then_inc(mean_ready, 1)
                dve.wait_ge(mean_ready, t + 1)
                nc.vector.tensor_scalar(var[s][:], mv[s][:, 1:2], LN1_EPS, None, ALU.add).then_inc(var_ready, 1)
                dve.wait_ge(rstd_ready, t + 1)
                if not first:
                    dve.wait_ge(turned, t - 1)
                nc.vector.tensor_scalar(xn[s][:], x[s][:], mv[s][:, 0:1], rstd[s][:], ALU.subtract, ALU.mult).then_inc(normed, 1)

            def low(j, s, first):
                t = 2 * j + s
                dve.wait_ge(xt_ready, t + 1)
                dve.wait_ge(hi_ready, t + 1)
                if not first:
                    dve.wait_ge(v_prod, t - 1)
                nc.vector.tensor_tensor(xtl[s][:], xt[s][:], xth[s][:].bitcast(F32), ALU.subtract).then_inc(lo_ready, 1)

            def bias(j, s, first):
                t = 2 * j + s
                dve.wait_ge(v_prod, t + 1)
                if not first:
                    dve.wait_ge(v_stored[s], 16 * j)
                for n in range(2):
                    c = slice(n * 512, (n + 1) * 512)
                    nc.vector.tensor_tensor(v[s][:, c], psV[s][n][:], bvb[:, c], ALU.add).then_inc(v_pre, 1)

            norm(0, 0, True)
            norm(0, 1, True)
            low(0, 0, True)
            low(0, 1, True)
            norm(1, 0, False)
            dve.wait_ge(b_loaded, 16)
            bias(0, 0, True)
            low(1, 0, False)
            norm(1, 1, False)
            bias(0, 1, True)
            low(1, 1, False)
            with dve.Fori(1, PAIRS - 1) as j:
                for s in range(2):
                    norm(j + 1, s, False)
                    bias(j, s, False)
                    low(j + 1, s, False)
            for s in range(2):
                bias(PAIRS - 1, s, False)

        @block.tensor
        def _(pe):
            def turn(j, s, first):
                t = 2 * j + s
                pe.wait_ge(normed, t + 1)
                if not first:
                    pe.wait_ge(hi_ready, t - 1)
                    pe.wait_ge(xt_ready, t - 1)
                for k in range(EC):
                    mm = nc.tensor.transpose(psT[s][:, k * P:(k + 1) * P], xn[s][:, k * P:(k + 1) * P], ident[:])
                mm.then_inc(turned, 1)

            def project(j, s, first):
                t = 2 * j + s
                pe.wait_ge(lo_ready, t + 1)
                if not first:
                    pe.wait_ge(v_pre, 2 * (t - 1))
                parts = [(xth[s], wvh), (xth[s], wvl), (xtl[s], wvh)]
                for n in range(2):
                    for k in range(EC):
                        for i, (a, b) in enumerate(parts):
                            mm = nc.tensor.matmul(psV[s][n][:], a[:, k * P:(k + 1) * P], b[:, k, n * 512:(n + 1) * 512],
                                                  start=(k == 0 and i == 0), stop=(k == EC - 1 and i == 2))
                mm.then_inc(v_prod, 1)

            turn(0, 0, True)
            turn(0, 1, True)
            project(0, 0, True)
            turn(1, 0, False)
            project(0, 1, True)
            turn(1, 1, False)
            with pe.Fori(1, PAIRS - 1) as j:
                for s in range(2):
                    project(j, s, False)
                    turn(j + 1, s, False)
            for s in range(2):
                project(PAIRS - 1, s, False)

        @block.scalar
        def _(act):
            def high(j, s, first):
                t = 2 * j + s
                act.wait_ge(turned, t + 1)
                if not first:
                    act.wait_ge(xt_stored[s], 16 * j)
                    act.wait_ge(lo_ready, t - 1)
                nc.scalar.copy(xt[s][:], psT[s][:]).then_inc(xt_ready, 1)
                if not first:
                    act.wait_ge(v_prod, t - 1)
                nc.scalar.copy(xth[s][:], psT[s][:]).then_inc(hi_ready, 1)

            def store_xt(j, s):
                t = 2 * j + s
                act.wait_ge(xt_ready, t + 1)
                act.dma_start(env.xt_dram[bass.ds(t, 1)].rearrange("o p c -> (o p) c"), xt[s][:]).then_inc(xt_stored[s], 16)

            def silu(j, s, first):
                t = 2 * j + s
                act.wait_ge(v_pre, 2 * (t + 1))
                nc.scalar.activation(v[s][:], v[s][:], ACT.Silu).then_inc(v_act, 1)
                act.wait_ge(v_act, t + 1)
                act.dma_start(pair_rows(env.v_dram, j, s), v[s][:]).then_inc(v_stored[s], 16)

            act.wait_ge(const_set, 1)
            nc.scalar.activation(warm[:], minus_half[:], ACT.Silu)
            for s in range(2):
                high(0, s, True)
                store_xt(0, s)
            with act.Fori(1, PAIRS) as j:
                for s in range(2):
                    high(j, s, False)
                    store_xt(j, s)
                    silu(j - 1, s, False)
            for s in range(2):
                silu(PAIRS - 1, s, False)
            for s in range(2):
                act.wait_ge(v_stored[s], 16 * PAIRS)
                act.wait_ge(xt_stored[s], 16 * PAIRS)


def load_xt(sp, env, g, nt):
    sp.dma_start(env.xt[:, 0:nt, :], env.xt_dram[bass.ds(g * GT, nt)].rearrange("i p c -> p i c")).then_inc(env.xt_loaded, 16)


def load_v(sp, nc, env, j, s, piece, bounds=MORE_PIECES):
    b0, b1 = bounds[piece:piece + 2]
    for kh in range(2):
        src = env.v_dram.rearrange("(b q) c -> q b c", q=POS)[
            kh * HALF:(kh + 1) * HALF, b0:b1, bass.ds((2 * j + s) * VC, VC)]
        sp.dma_start(env.v[s][:, kh, b0:b1, :], src).then_inc(env.v_loaded[s], 16)


def load_T(sp, nc, env, n, par):
    for p in range(ROWS_HALF):
        src = env.a_rows[bass.ds(n, 1), p]
        sp.dma_start(env.T[par][p * SIDE:(p + 1) * SIDE].rearrange("q (r s) c -> q r (s c)", r=TROWS),
                     src.rearrange("o q r f -> (o q) r f")).then_inc(env.T_loaded[par], 16)


def token_pairs(rows, g, nt):
    return rows[bass.ds(g * GT * P, nt * P), :].rearrange("(t p e) c -> p t (e c)", p=P, e=2)


def in_pairs(t, nt):
    return t[:, 0:nt, :].rearrange("p (t e) c -> p t (e c)", e=2)


def convolve(nc, d, env):
    VCH = D // VC
    TPV = VC // CC
    HQ = CC // 2
    BANKS = HQ // 2
    EARLY = 2
    with ExitStack() as ctx:
        sb = lambda n, s, t=F32: ctx.enter_context(nc.sbuf_tensor(n, s, t))
        sem = lambda n: ctx.enter_context(nc.semaphore(n))
        env.v.append(sb("vB1", [HALF, 2, IMAGES, VC]))
        v, T, v_loaded, T_loaded = env.v, env.T, env.v_loaded, env.T_loaded
        y = [sb(f"yB{i}", [P, HQ, POS]) for i in range(2)]
        ps = [ctx.enter_context(nc.psum_tensor(f"psB{i}", [P, 512], F32)) for i in range(2 * BANKS)]
        y_stored = [sem(f"yB_stored{i}") for i in range(2)]
        bank_ready, out_dve, out_act = sem("bank_ready"), sem("y_out_dve"), sem("y_out_act")
        block = ctx.enter_context(nc.Block())

        @block.sync
        def _(sp):
            def store_y(n, par):
                for h in range(2):
                    dst = env.y_dram.rearrange("(n h q) (b p) -> n h b q p", h=2, q=HQ, p=POS)[bass.ds(n, 1), h]
                    sp.dma_start(dst.rearrange("o b q p -> (o b) q p"), y[par][h * IMAGES:(h + 1) * IMAGES]).then_inc(y_stored[par], 16)

            def chunk(j, s, tt, first, last):
                n = 2 * TPV * j + TPV * s + tt
                if not (first and n < 2):
                    sp.wait_ge(bank_ready, BANKS * (n - 1))
                    load_T(sp, nc, env, n, tt % 2)
                if 2 <= tt < 2 + V_PIECES:
                    if s == 0:
                        if not (first and tt - 2 < EARLY):
                            load_v(sp, nc, env, j, 1, tt - 2)
                    elif not last:
                        load_v(sp, nc, env, j + 1, 0, tt - 2)
                if not (first and n < 2):
                    sp.wait_ge(out_dve, BANKS // 2 * (n - 1))
                    sp.wait_ge(out_act, BANKS // 2 * (n - 1))
                    store_y(n - 2, tt % 2)

            for piece in range(EARLY):
                load_v(sp, nc, env, 0, 1, piece)
            for s in range(2):
                for tt in range(TPV):
                    chunk(0, s, tt, True, False)
            with sp.Fori(1, VCH // 2 - 1) as j:
                for s in range(2):
                    for tt in range(TPV):
                        chunk(j, s, tt, False, False)
            for s in range(2):
                for tt in range(TPV):
                    chunk(VCH // 2 - 1, s, tt, False, True)
            for n in (CHUNKS - 2, CHUNKS - 1):
                sp.wait_ge(out_dve, BANKS // 2 * (n + 1))
                sp.wait_ge(out_act, BANKS // 2 * (n + 1))
                store_y(n, n % 2)
            for s in range(2):
                sp.wait_ge(y_stored[s], 16 * CHUNKS)

        @block.tensor
        def _(pe):
            def chunk(j, s, tt, first):
                n = 2 * TPV * j + TPV * s + tt
                par = tt % 2
                if tt == 0:
                    pe.wait_ge(v_loaded[s], 2 * V_PIECES * 16 * (j + 1))
                pe.wait_ge(T_loaded[par], ROWS_HALF * 16 * (TPV * j + TPV // 2 * s + tt // 2 + 1))
                for h in range(2):
                    for qq in range(BANKS):
                        bank = ps[par * BANKS + qq]
                        if h == 0 and not (first and n < 2):
                            pe.wait_ge(out_dve if qq % 2 == 0 else out_act, BANKS // 2 * (n - 2) + qq // 2 + 1)
                        for q in (2 * qq, 2 * qq + 1):
                            for kh in range(2):
                                c = h * HQ + q
                                mm = nc.tensor.matmul(bank[h * IMAGES:(h + 1) * IMAGES, (q % 2) * POS:(q % 2 + 1) * POS],
                                                      v[s][:, kh, :, tt * CC + c],
                                                      T[par][:, kh * HALF:kh * HALF + POS, c],
                                                      start=(kh == 0), stop=(kh == 1))
                        if h == 1:
                            mm.then_inc(bank_ready, 1)

            for s in range(2):
                for tt in range(TPV):
                    chunk(0, s, tt, True)
            with pe.Fori(1, VCH // 2) as j:
                for s in range(2):
                    for tt in range(TPV):
                        chunk(j, s, tt, False)

        def evacuate(eng, copy, done, odd):
            def chunk(j, s, tt, first):
                n = 2 * TPV * j + TPV * s + tt
                par = tt % 2
                if not (first and n < 2):
                    eng.wait_ge(y_stored[par], 32 * (TPV * j + TPV // 2 * s + tt // 2))
                for qq in range(odd, BANKS, 2):
                    eng.wait_ge(bank_ready, BANKS * n + qq + 1)
                    copy(y[par][:, 2 * qq:2 * qq + 2, ::-1],
                         ps[par * BANKS + qq][:, 0:2 * POS].rearrange("p (q n) -> p q n", q=2)).then_inc(done, 1)

            for s in range(2):
                for tt in range(TPV):
                    chunk(0, s, tt, True)
            with eng.Fori(1, VCH // 2) as j:
                for s in range(2):
                    for tt in range(TPV):
                        chunk(j, s, tt, False)

        @block.vector
        def _(dve):
            evacuate(dve, nc.vector.tensor_copy, out_dve, 0)

        @block.scalar
        def _(act):
            evacuate(act, nc.scalar.copy, out_act, 1)


def groups(nc, d, env):
    G = GT * P
    GP = G // 2
    YR, HR = 4, 3
    SPLIT_AT = HC - 2 * GT
    with ExitStack() as ctx:
        sb = lambda n, s, t=F32: ctx.enter_context(nc.sbuf_tensor(n, s, t))
        psum = lambda n: ctx.enter_context(nc.psum_tensor(n, [P, 512], F32))
        sem = lambda n: ctx.enter_context(nc.semaphore(n))
        ident = env.ident
        xt, xt_loaded = env.xt, env.xt_loaded
        bu, b1 = sb("bu", [P, DC]), sb("b1", [P, HC])
        bo, b2 = sb("bo", [P, E]), sb("b2", [P, LL])
        minus_half = sb("minus_half", [P, GT])
        step_in, half_col, warm = sb("step_in", [P, 1]), sb("half_col", [P, 1]), sb("warm", [P, 2])
        x, x1, r = (sb(n, [P, GT, E]) for n in ("x", "x1", "r"))
        s, s4 = sb("s", [P, GT, LL]), sb("s4", [P, GT // 2, LL])
        xth, xtl = sb("xth", [P, EC, G], F32R), sb("xtl", [P, EC, G], F32R)
        y = sb("y", [P, YR, G])
        u = sb("u", [P, 2, G])
        zh, zl = sb("zh", [P, 2, G], F32R), sb("zl", [P, 2, G], F32R)
        llh, lll = sb("llh", [P, LC, GP], F32R), sb("lll", [P, LC, GP], F32R)
        hf = sb("hf", [P, 2, GP])
        hh, hl = sb("hh", [P, HR, GP], F32R), sb("hl", [P, HR, GP], F32R)
        lln = sb("lln", [P, 2, LL])
        stat, mv, var, rstd = (sb(n, sh) for n, sh in (("stat", [P, GT, 6]), ("mv", [P, GT, 2]), ("var", [P, GT]), ("rstd", [P, GT])))
        acc = [psum(f"acc{i}") for i in range(GT)]
        work = [psum(f"work{i}") for i in range(2)]
        ffn = [psum(f"ffn{i}") for i in range(2)]
        const_loaded, half_set, b2_halved = sem("const_loaded"), sem("half_set"), sem("b2_halved")
        x_loaded, out_stored = sem("x_loaded"), sem("out_stored")
        y_loaded = [sem(f"y_loaded{i}") for i in range(YR)]
        stats_ready, means_ready, var_ready, rstd_ready = (sem(n) for n in ("stats_ready", "means_ready", "var_ready", "rstd_ready"))
        xth_ready, xtl_ready, bo_added = (sem(n) for n in ("xth_ready", "xtl_ready", "bo_added"))
        u_prod, u_ready, z_made, zh_ready, zl_ready, wo_used, acc_ready = (
            sem(n) for n in ("u_prod", "u_ready", "z_made", "zh_ready", "zl_ready", "wo_used", "acc_ready"))
        x1_ready, xn2_ready, s_ready, r_ready = (sem(n) for n in ("x1_ready", "xn2_ready", "s_ready", "r_ready"))
        ll_prod, llh_ready, lll_ready = sem("ll_prod"), sem("llh_ready"), sem("lll_ready")
        h_prod, h_act, hl_ready, h_used = sem("h_prod"), sem("h_act"), sem("hl_ready"), sem("h_used")
        s4_ready, rest_ready, lln_ready, out_ready = sem("s4_ready"), sem("rest_ready"), sem("lln_ready"), sem("out_ready")
        warmed, col_set = sem("warmed"), sem("col_set")
        staged = [sem(f"w_staged{i}") for i in range(2)]
        w_hi, w_lo = sem("w_hi"), sem("w_lo")
        block = ctx.enter_context(nc.Block())
        x_rows = d["x"]
        out_rows = d["out"]
        CONSTS = 4

        pieces = []
        for src, (hi, lo) in ((d["L0_conv_Wo"], env.wo), (env.w1_dram, env.w1), (d["fc2_wT"], env.w2)):
            src = src.rearrange("(k p) n -> p k n", p=P)
            for i in range(2):
                k = slice(i * src.shape[1] // 2, (i + 1) * src.shape[1] // 2)
                pieces.append((src[:, k, :], hi[:, k, :], lo[:, k, :]))
        WO = 2

        def stage(i):
            k = pieces[i][0].shape[1]
            return (x1, r)[i % 2].rearrange("p i c -> p (i c)").rearrange("p (k n) -> p k n", k=k)

        def tiles(g):
            return max(0, min(GT, TILES - GT * g)) if g >= 0 else 0

        def halves(g, cur, m):
            return GT // 2 * DC * g + cur // 2 * m

        def iterations(eng, step):
            for g in range(3):
                step(g, tiles(g), tiles(g - 1), tiles(g - 2), tiles(g + 1), g)
            with eng.Fori(3, GROUPS - 2) as g:
                step(g, GT, GT, GT, GT, 3)
            for g in range(GROUPS - 2, GROUPS + 2):
                step(g, tiles(g), tiles(g - 1), tiles(g - 2), tiles(g + 1), 3)

        @block.sync
        def _(sp):
            def load_constants():
                for t, name in ((bu, "bu"), (b1, "b1")):
                    sp.dma_start(t[:], d[name]).then_inc(const_loaded, 16)
                for t, name, n in ((bo, "L0_conv_bo", E), (b2, "L0_ffn_fc2_b", LL)):
                    sp.dma_start(t[:], bass.AP(d[name].tensor, 0, [[0, P], [1, n]])).then_inc(const_loaded, 16)

            def load_x(g, nt):
                sp.dma_start(in_pairs(x, nt), token_pairs(x_rows, g, nt)).then_inc(x_loaded, 16)

            def load_y(g, m, nt):
                sp.dma_start(y[:, m % YR, 0:nt * P], env.y_dram[m * P:(m + 1) * P, bass.ds(g * G, nt * P)]).then_inc(y_loaded[m % YR], 16)

            for i, (src, _, _) in enumerate(pieces):
                if i == WO:
                    load_constants()
                    load_x(0, GT)
                    for m in range(YR):
                        load_y(0, m, GT)
                if i >= 2:
                    sp.wait_ge(w_lo, i - 1)
                sp.dma_start(stage(i), src).then_inc(staged[i % 2], 16)

            def step(g, cur, prev, last, nxt, age):
                if last:
                    sp.wait_ge(out_ready, GT // 2 * (g - 2) + last // 2)
                    result = r if prev else xt
                    sp.dma_start(token_pairs(out_rows, g - 2, last), in_pairs(result, last)).then_inc(out_stored, 16)
                if nxt:
                    sp.wait_ge(xtl_ready, GT * g + cur)
                    load_xt(sp, env, g + 1, nxt)
                if cur:
                    for m in range(YR, DC):
                        sp.wait_ge(z_made, halves(g, cur, m - YR + 1))
                        load_y(g, m, cur)
                if nxt:
                    sp.wait_ge(bo_added, GT * g + cur)
                    load_x(g + 1, nxt)
                    for m in range(YR):
                        sp.wait_ge(z_made, halves(g, cur, m + YR + 1))
                        load_y(g + 1, m, nxt)

            iterations(sp, step)
            sp.wait_ge(out_stored, 16 * GROUPS)

        @block.gpsimd
        def _(pool):
            nc.gpsimd.memset(minus_half[:], -0.5).then_inc(half_set, 1)
            pool.wait_ge(half_set, 1)

            def second_root(g, nt):
                pool.wait_ge(var_ready, g + 1)
                nc.gpsimd.tensor_tensor(rstd[:, 0:nt], var[:, 0:nt], minus_half[:, 0:nt], ALU.pow).then_inc(rstd_ready, 1)

            def sum_four(g, i, again):
                pool.wait_ge(s_ready, GT * g + i + 1)
                if again:
                    pool.wait_ge(rest_ready, g)
                nc.gpsimd.tensor_tensor(s4[:, i // 2, :], s[:, i - 1, :], s[:, i, :], ALU.add).then_inc(s4_ready, 1)

            pool.wait_ge(const_loaded, 16 * CONSTS)

            def step(g, cur, prev, last, nxt, age):
                if cur and prev:
                    second_root(g - 1, prev)
                for i in range(GT):
                    if cur and i % 2 and i < prev:
                        sum_four(g - 1, i, age >= 2)
                    if i < cur:
                        if i == 0:
                            pool.wait_ge(x_loaded, 16 * (g + 1))
                            if age == 0:
                                pool.wait_ge(w_lo, len(pieces) - 1)
                        if prev:
                            pool.wait_ge(r_ready, GT * (g - 1) + i + 1)
                        nc.gpsimd.tensor_tensor(x1[:, i, :], x[:, i, :], bo[:], ALU.add).then_inc(bo_added, 1)
                if cur and not nxt:
                    second_root(g, cur)
                    for i in range(1, cur, 2):
                        sum_four(g, i, True)

            iterations(pool, step)

        @block.tensor
        def _(pe):
            def three(out, a, b, first, last):
                for i, (p, q) in enumerate(((0, 0), (0, 1), (1, 0))):
                    mm = nc.tensor.matmul(out, a[p], b[q], start=(first and i == 0), stop=(last and i == 2))
                return mm

            def step(g, cur, prev, last, nxt, age):
                n, pairs = cur * P, prev * P // 2

                def make_u(m):
                    if m == 0:
                        pe.wait_ge(xtl_ready, GT * g + cur)
                    if m >= 2:
                        pe.wait_ge(u_ready, DC * g + m - 1)
                    elif age >= 2:
                        pe.wait_ge(h_act, 2 * HC * (g - 1))
                    for k in range(EC):
                        c = slice(m * P, (m + 1) * P)
                        mm = three(work[m % 2][:, 0:n], [w[:, k, c] for w in env.wu], [t[:, k, 0:n] for t in (xth, xtl)],
                                   k == 0, k == EC - 1)
                    mm.then_inc(u_prod, 1)

                def make_ll():
                    pe.wait_ge(s4_ready, GT // 2 * (g - 1) + prev // 2)
                    if age >= 2:
                        pe.wait_ge(lln_ready, g - 1)
                    for t in range(prev // 2):
                        for c in range(LC):
                            mm = nc.tensor.transpose(ffn[1][:, c * GP + t * P:c * GP + (t + 1) * P],
                                                     s4[:, t, c * P:(c + 1) * P], ident[:])
                    mm.then_inc(ll_prod, 1)

                def use_z(q):
                    if age == 0 and q == 0:
                        pe.wait_ge(w_lo, WO)
                    for i in range(cur):
                        if i % 2 == 0:
                            pe.wait_ge(zl_ready, halves(g, cur, q) + i // 2 + 1)
                        if age and q == 0:
                            pe.wait_ge(x1_ready, GT * (g - 1) + i + 1)
                        t = slice(i * P, (i + 1) * P)
                        mm = three(acc[i][:], [z[:, q % 2, t] for z in (zh, zl)], [w[:, q, :] for w in env.wo], q == 0, q == DC - 1)
                        if q == DC - 1:
                            mm.then_inc(acc_ready, 1)
                        elif i == cur - 1:
                            mm.then_inc(wo_used, 1)

                def make_h(m):
                    if age == 1 and m == 0:
                        pe.wait_ge(w_lo, len(pieces))
                    if m == 0:
                        pe.wait_ge(lll_ready, g)
                    if m >= 2:
                        pe.wait_ge(h_act, 2 * (HC * (g - 1) + m - 1))
                    elif cur:
                        pe.wait_ge(u_ready, DC * g + DC - 1 + m)
                    else:
                        pe.wait_ge(h_act, 2 * HC * (g - 1))
                    for k in range(LC):
                        c = slice(m * P, (m + 1) * P)
                        mm = three(work[m % 2][:, 0:pairs], [w[:, k, c] for w in env.w1], [t[:, k, 0:pairs] for t in (llh, lll)],
                                   k == 0, k == LC - 1)
                    mm.then_inc(h_prod, 1)

                def use_h(q):
                    pe.wait_ge(hl_ready, HC * (g - 1) + q + 1)
                    for t in range(prev // 2):
                        c = slice(t * P, (t + 1) * P)
                        mm = three(ffn[t][:, 0:LL], [h[:, q % HR, c] for h in (hh, hl)], [w[:, q, :] for w in env.w2],
                                   q == 0, q == HC - 1)
                    mm.then_inc(h_used, 1)

                for m in range(DC):
                    if cur:
                        make_u(m)
                    if prev and m == DC - 2:
                        make_ll()
                    if cur and m >= 1:
                        use_z(m - 1)
                if prev:
                    make_h(0)
                    make_h(1)
                if cur:
                    use_z(DC - 1)
                for m in range(2, HC):
                    if prev:
                        make_h(m)
                        use_h(m - 2)
                if prev:
                    use_h(HC - 2)
                    use_h(HC - 1)

            iterations(pe, step)

        @block.scalar
        def _(act):
            def high(g, i):
                if i == 0:
                    act.wait_ge(xt_loaded, 16 * (g + 1))
                nc.scalar.copy(xth[:, :, i * P:(i + 1) * P], xt[:, i, :].rearrange("p (k t) -> p k t", k=EC)).then_inc(xth_ready, 1)

            def split_high(i):
                act.wait_ge(staged[i % 2], 16 * (i // 2 + 1))
                nc.scalar.copy(pieces[i][1], stage(i)).then_inc(w_hi, 1)

            for i in range(GT):
                high(0, i)
            for i in range(WO):
                split_high(i)
            act.wait_ge(const_loaded, 16 * CONSTS)
            act.wait_ge(col_set, 1)

            def high_ll(g, pairs):
                act.wait_ge(ll_prod, g)
                nc.scalar.copy(llh[:, :, 0:pairs], ffn[1][:].rearrange("p (c t) -> p c t", c=LC)[:, :, 0:pairs]).then_inc(llh_ready, 1)

            def step(g, cur, prev, last, nxt, age):
                n, pairs = cur * P, prev * P // 2
                if cur:
                    for m in range(DC):
                        act.wait_ge(u_prod, DC * g + m + 1)
                        if age or m >= 2:
                            act.wait_ge(zl_ready, halves(g, cur, m - 1) if m >= 2 else GT // 2 * (DC * g + m - 1))
                        nc.scalar.activation(u[:, m % 2, 0:n], work[m % 2][:, 0:n], ACT.Silu, bias=bu[:, m:m + 1]).then_inc(u_ready, 1)
                        if age == 0 and WO + m < len(pieces):
                            split_high(WO + m)
                        if prev and m == DC - 2:
                            high_ll(g, pairs)
                if prev:
                    if not cur:
                        high_ll(g, pairs)
                    nc.scalar.activation(warm[:, 1:2], half_col[:], ACT.Gelu).then_inc(warmed, 1)
                for m in range(HC):
                    if 0 <= m - SPLIT_AT < nxt:
                        high(g + 1, m - SPLIT_AT)
                    if prev:
                        act.wait_ge(h_prod, HC * (g - 1) + m + 1)
                        if age >= 2 or m >= 2:
                            act.wait_ge(hl_ready, HC * (g - 1) + m - 1)
                        if age >= 2 or m >= HR:
                            act.wait_ge(h_used, HC * (g - 1) + m - HR + 1)
                        for dst in (hf[:, m % 2, 0:pairs], hh[:, m % HR, 0:pairs]):
                            nc.scalar.activation(dst, work[m % 2][:, 0:pairs], ACT.Gelu, bias=b1[:, m:m + 1]).then_inc(h_act, 1)
                if nxt:
                    nc.scalar.activation(warm[:, 0:1], half_col[:], ACT.Silu).then_inc(warmed, 1)

            iterations(act, step)

        @block.vector
        def _(dve):

            def statistics(lo, hi):
                for i in range(lo, hi):
                    nc.vector.bn_stats(stat[:, i, :], x1[:, i, :]).then_inc(stats_ready, 1)

            def variances(g, nt):
                dve.wait_ge(stats_ready, GT * g + nt)
                nc.vector.memset(step_in[:], 0.0)
                for i in range(nt):
                    nc.vector.bn_aggr(mv[:, i, :], stat[:, i, :]).then_inc(means_ready, 1)
                dve.wait_ge(means_ready, GT * g + nt)
                nc.vector.tensor_scalar(var[:, 0:nt], mv[:, 0:nt, 1], LN2_EPS, None, ALU.add).then_inc(var_ready, 1)

            def low(g, i):
                dve.wait_ge(xth_ready, GT * g + i + 1)
                t = slice(i * P, (i + 1) * P)
                nc.vector.tensor_tensor(xtl[:, :, t], xt[:, i, :].rearrange("p (k t) -> p k t", k=EC),
                                        xth[:, :, t].bitcast(F32), ALU.subtract).then_inc(xtl_ready, 1)

            def second_norm(g, i, age, result):
                if i == 0:
                    dve.wait_ge(rstd_ready, g + 1)
                    if age >= 2:
                        dve.wait_ge(s4_ready, GT // 2 * g)
                        if result is r:
                            dve.wait_ge(out_stored, 16 * g)
                        else:
                            dve.wait_ge(xtl_ready, GT * g + tiles(GROUPS - 1))
                nc.vector.tensor_scalar(result[:, i, :], x1[:, i, :], mv[:, i, 0:1], rstd[:, i:i + 1],
                                        ALU.subtract, ALU.mult).then_inc(xn2_ready, 1)
                dve.wait_ge(xn2_ready, GT * g + i + 1)
                even_odd = result[:, i, :].rearrange("p (c e) -> p c e", e=2)
                nc.vector.tensor_tensor(s[:, i, :], even_odd[:, :, 0], even_odd[:, :, 1], ALU.add).then_inc(s_ready, 1)
                dve.wait_ge(s_ready, GT * g + i + 1)
                nc.vector.tensor_tensor(result[:, i, :], result[:, i, :], x1[:, i, :], ALU.add).then_inc(r_ready, 1)

            def split_low(i):
                dve.wait_ge(w_hi, i + 1)
                nc.vector.tensor_tensor(pieces[i][2], stage(i), pieces[i][1].bitcast(F32), ALU.subtract).then_inc(w_lo, 1)

            for i in range(GT):
                low(0, i)
            for i in range(WO):
                split_low(i)
            nc.vector.memset(half_col[:], 0.5).then_inc(col_set, 1)
            dve.wait_ge(const_loaded, 16 * CONSTS)
            nc.vector.tensor_scalar(b2[:], b2[:], 0.5, None, ALU.mult).then_inc(b2_halved, 1)
            dve.wait_ge(b2_halved, 1)

            def first_sum(g, i):
                dve.wait_ge(acc_ready, GT * g + i + 1)
                dve.wait_ge(bo_added, GT * g + i + 1)
                nc.vector.tensor_tensor(x1[:, i, :], acc[i][:], x1[:, i, :], ALU.add).then_inc(x1_ready, 1)

            SECOND_NORM_AT = {3: (0, 1), 4: (2,), 5: (3,)}
            LAST_NORM_AT = 4

            def add_sum(g, t, r):
                blocks = r[:, 2 * t:2 * t + 2, :].rearrange("p e (c w) -> p e c w", w=2)
                add = lln[:, t, :].unsqueeze(1).unsqueeze(3).broadcast_to([P, 2, LL, 2])
                nc.vector.tensor_tensor(blocks, blocks, add, ALU.add).then_inc(out_ready, 1)

            def step(g, cur, prev, last, nxt, age):
                n, pairs = cur * P, prev * P // 2
                for m in range(DC):
                    if m < last // 2:
                        if m == 0:
                            dve.wait_ge(lln_ready, g - 1)
                            dve.wait_ge(r_ready, GT * (g - 2) + last)
                        add_sum(g - 2, m, r if prev else xt)
                    if cur:
                        dve.wait_ge(u_ready, DC * g + m + 1)
                        dve.wait_ge(y_loaded[m % YR], 16 * (DC // YR * g + m // YR + 1))
                        if m >= 2:
                            dve.wait_ge(wo_used, (DC - 1) * g + m - 1)
                        elif age:
                            dve.wait_ge(acc_ready, GT * g)
                        for t in range(cur // 2):
                            c = slice(2 * t * P, 2 * (t + 1) * P)
                            z = u[:, m % 2, c]
                            nc.vector.tensor_tensor(z.rearrange("c (e p) -> c e p", e=2), z.rearrange("c (e p) -> c e p", e=2),
                                                    y[:, m % YR, c].rearrange("c (p e) -> c e p", e=2), ALU.mult).then_inc(z_made, 1)
                            dve.wait_ge(z_made, halves(g, cur, m) + t + 1)
                            nc.vector.tensor_copy(zh[:, m % 2, c], z).then_inc(zh_ready, 1)
                            dve.wait_ge(zh_ready, halves(g, cur, m) + t + 1)
                            nc.vector.tensor_tensor(zl[:, m % 2, c], z, zh[:, m % 2, c].bitcast(F32), ALU.subtract).then_inc(zl_ready, 1)
                        if age == 0 and WO + m < len(pieces):
                            split_low(WO + m)
                    if prev and cur:
                        if 0 < m < 3:
                            dve.wait_ge(x1_ready, GT * (g - 1) + prev)
                            statistics(2 * m - 2, min(2 * m, prev))
                            if m == 2:
                                variances(g - 1, prev)
                        elif m in SECOND_NORM_AT:
                            for i in SECOND_NORM_AT[m]:
                                if i < prev:
                                    second_norm(g - 1, i, age, r)
                    if prev:
                        if m == DC - 2:
                            dve.wait_ge(llh_ready, g)
                            nc.vector.tensor_tensor(lll[:, :, 0:pairs], ffn[1][:].rearrange("p (c t) -> p c t", c=LC)[:, :, 0:pairs],
                                                    llh[:, :, 0:pairs].bitcast(F32), ALU.subtract).then_inc(lll_ready, 1)
                            if last:
                                dve.wait_ge(out_ready, GT // 2 * (g - 1))
                            for t in range(prev // 2):
                                ins = nc.vector.scalar_tensor_tensor(out=lln[:, t, :], in0=s4[:, t, :], scalar=-0.25, in1=b2[:],
                                                                     op0=ALU.mult, op1=ALU.add)
                            ins.then_inc(rest_ready, 1)
                for m in range(HC):
                    if prev:
                        dve.wait_ge(h_act, 2 * (HC * (g - 1) + m + 1))
                        if age >= 2 or m >= HR:
                            dve.wait_ge(h_used, HC * (g - 1) + m - HR + 1)
                        nc.vector.tensor_tensor(hl[:, m % HR, 0:pairs], hf[:, m % 2, 0:pairs], hh[:, m % HR, 0:pairs].bitcast(F32),
                                                ALU.subtract).then_inc(hl_ready, 1)
                    if m < cur:
                        first_sum(g, m)
                    if cur and not nxt:
                        if m == LAST_NORM_AT:
                            dve.wait_ge(x1_ready, GT * g + cur)
                            statistics(0, cur)
                        elif m == LAST_NORM_AT + 1:
                            variances(g, cur)
                        elif 0 <= m - (LAST_NORM_AT + 2) < cur:
                            second_norm(g, m - (LAST_NORM_AT + 2), age, xt)
                    if 0 <= m - SPLIT_AT < nxt:
                        low(g + 1, m - SPLIT_AT)
                if prev:
                    dve.wait_ge(h_used, HC * g)
                    dve.wait_ge(rest_ready, g)
                    for t in range(prev // 2):
                        ins = nc.vector.scalar_tensor_tensor(out=lln[:, t, :], in0=ffn[t][:, 0:LL], scalar=0.5, in1=lln[:, t, :],
                                                             op0=ALU.mult, op1=ALU.add)
                    ins.then_inc(lln_ready, 1)

            iterations(dve, step)


def metaformer(nc, d):
    env = Env()
    env.a_dram = nc.dram_tensor("rel_kernel", [CHUNKS, NREL, CC], F32).ap()
    env.v_dram = nc.dram_tensor("v_scratch", [TOKENS, D], F32).ap()
    env.y_dram = nc.dram_tensor("y_scratch", [D, TOKENS], F32).ap()
    env.a_rows = bass.AP(env.a_dram.tensor, 0, [[NREL * CC, CHUNKS], [REL * CC, ROWS_HALF], [CC, SIDE], [REL * CC, TROWS], [1, SIDE * CC]])
    env.xt_dram = nc.dram_tensor("xt_scratch", [TILES, P, E], F32).ap()
    env.w1_dram = nc.dram_tensor("w1_scratch", [LL, HID], F32).ap()
    with ExitStack() as ctx:
        sem = lambda n: ctx.enter_context(nc.semaphore(n))
        env.a_stored, env.w1_stored = sem("a_stored"), sem("w1_stored")
        env.v_loaded, env.T_loaded = ([sem(f"{n}_loaded{i}") for i in range(2)] for n in ("v", "T"))
        env.xt_loaded = sem("xt_loaded")
        env.xA_loaded = [sem(f"xA_loaded{i}") for i in range(2)]
        parts = lambda n, s, **side: [ctx.enter_context(nc.sbuf_tensor(f"{n}_{part}", s, F32R, **side)) for part in ("hi", "lo")]
        env.ident = ctx.enter_context(nc.sbuf_tensor("ident", [P, P], F32, side="right"))
        with ExitStack() as first:
            shared = env.shared = first.enter_context(nc.sbuf_tensor("v_chunk0", [P, 2 * IMAGES * VC], F32))
            place = lambda at, n: shared[:, at:at + n]
            env.a_tile = place(0, OT * D).rearrange("p (t n) -> p t n", n=D)
            env.w1_tile = place(OT * D, LC * HID).rearrange("p (i n) -> p i n", n=512)
            env.wv_stage = place(OT * D + LC * HID, EC * D).rearrange("p (k n) -> p k n", n=D)
            env.fc1_place = place(OT * D + LC * HID + EC * D, HID)
            env.v = [shared[0:HALF, :].rearrange("p (h b c) -> p h b c", h=2, c=VC)]
            with ExitStack() as second:
                env.wv = [second.enter_context(nc.sbuf_tensor(n, [P, EC, D], F32R)) for n in ("wv_hi", "wv_lo")]
                env.xA = [second.enter_context(nc.sbuf_tensor(f"xA{i}", [P, E], F32)) for i in range(2)]
                rel_mlp(nc, d, env)
                env.xt = ctx.enter_context(nc.sbuf_tensor("xt", [P, GT, E], F32, side="right"))
                env.wu = parts("wu", [P, EC, D], side="right")
                env.T = [first.enter_context(nc.sbuf_tensor(f"T{i}", [HALF, TROWS * SIDE, CC], F32, side="right")) for i in range(2)]
                values(nc, d, env)
            convolve(nc, d, env)
        env.wo = parts("wo", [P, DC, E])
        env.w1, env.w2 = parts("w1", [P, LC, HID]), parts("w2", [P, HC, LL])
        groups(nc, d, env)


def interpolation():
    at = np.linspace(0.0, 1.0, E, dtype=np.float32) * np.float32(LL - 1)
    i0 = np.clip(np.floor(at).astype(np.int32), 0, LL - 2)
    w = at - i0.astype(np.float32)
    interp = np.zeros((E, LL), np.float32)
    interp[np.arange(E), i0] = np.float32(1.0) - w
    interp[np.arange(E), i0 + 1] = w
    return interp


def constants():
    c = {"ident": np.eye(P, dtype=np.float32)}
    c["half_interpT"] = interpolation() * np.float32(0.5)
    away = (SIDE - 1 - np.arange(REL)).astype(np.float32)
    di, dj = np.meshgrid(away, away, indexing="ij")
    c["rel_pos"] = np.pad(np.stack([di.ravel(), dj.ravel(), np.ones(NREL, np.float32)]), ((0, 0), (0, W_REL - NREL)))
    g = np.float32(0.999) ** (np.abs(di) + np.abs(dj)).ravel()
    gamma = np.zeros(OT * P, np.float32)
    gamma[:NREL] = g
    c["rel_gamma"] = np.ascontiguousarray(gamma.reshape(OT, P).T)
    return c


def kernel(**inputs):
    import concourse.bacc as bacc
    from concourse.bass_utils import run_bass_kernel_spmd

    arrays = {name: np.ascontiguousarray(a) for name, a in inputs.items()}
    arrays["x"] = arrays["x"].reshape(TOKENS, E)
    cols = lambda a, n: np.ascontiguousarray(np.asarray(a).reshape(n, P).T)
    arrays["bu"] = cols(arrays.pop("L0_conv_bu"), DC)
    arrays["b1"] = cols(arrays.pop("L0_ffn_fc1_b"), HC)
    arrays["fc1_wT"] = np.ascontiguousarray(arrays.pop("L0_ffn_fc1_w").T)
    arrays["fc2_wT"] = np.ascontiguousarray(arrays.pop("L0_ffn_fc2_w").T)
    arrays.update(constants())
    nc = bacc.Bacc("TRN2", target_bir_lowering=False, num_devices=1, dynamic_dma_scratch_size=1024)
    d = {n: nc.dram_tensor("in_" + n, a.shape, mybir.dt.from_np(a.dtype), kind="ExternalInput").ap() for n, a in arrays.items()}
    d["out"] = nc.dram_tensor("out", (TOKENS, E), F32, kind="ExternalOutput").ap()
    metaformer(nc, d)
    r = run_bass_kernel_spmd(nc, [{"in_" + n: a for n, a in arrays.items()}], core_ids=[0])
    return r.results[0]["out"].reshape(IMAGES, SIDE, SIDE, E)
```
